# Optimizing a Trainium2 kernel written in Bass

```python
import numpy as np
import jax
import jax.numpy as jnp

def _softmax(x, axis=-1):
    return jax.nn.softmax(x, axis=axis)

def _gelu(x):
    return jax.nn.gelu(x, approximate=True)

def _silu(x):
    return jax.nn.silu(x)

def _sigmoid(x):
    return jax.nn.sigmoid(x)

def _layernorm(x, axis=-1, eps=1e-05):
    m = jnp.mean(x, axis=axis, keepdims=True)
    v = jnp.var(x, axis=axis, keepdims=True)
    return (x - m) / jnp.sqrt(v + eps)

def _scatter_add(tgt, idx, src, axis=0):
    return tgt.at[idx].add(src)

def _segment_sum(src, seg, n):
    return jax.ops.segment_sum(src, seg, n)
kernel_name = 'mk_xattn_ffn_d1_seqx_r8_ce7f29'

def setup_inputs(seed: int=0):
    np.random.seed(seed)
    _w = jnp.asarray

    def _rec_inputs():
        import jax
        import jax.numpy as jnp
        _rk = jax.random.key(seed)
        x = 7.22e-05 + 1 * jax.random.normal(jax.random.fold_in(_rk, 1), (8, 256, 128), jnp.float32)
        _lenS = 256 - jax.random.randint(jax.random.fold_in(_rk, 7), (8,), 0, max(1, 256 // 4) + 1, jnp.int32)
        _lenS2 = 256 - jax.random.randint(jax.random.fold_in(_rk, 8), (8,), 0, max(1, 256 // 4) + 1, jnp.int32)
        _ctx_1024P = jax.random.normal(jax.random.fold_in(_rk, 11), (8, 16, 128), jnp.float32)
        _ctx_1024c = jax.random.dirichlet(jax.random.fold_in(_rk, 511), 0.3 * jnp.ones((16,), jnp.float32), (8, 256))
        _ctx_1024t = jnp.einsum('bsk,bkd->bsd', _ctx_1024c, _ctx_1024P)
        _ctx_1024t = _ctx_1024t * jax.lax.rsqrt(jnp.mean(jnp.square(_ctx_1024t)) + 1e-12) * 0.953939
        ctx_1024 = 4.13588e-05 + 0.999923 * (_ctx_1024t + 0.3 * jax.random.normal(jax.random.fold_in(_rk, 611), (8, 256, 128), jnp.float32))
        return (x, ctx_1024)
    x, ctx_1024 = _rec_inputs()

    def _L0_xattn_setup():
        import jax, jax.numpy as jnp
        import numpy as np
        EMBED = 128
        HEADS = 16
        HEAD_DIM = EMBED // HEADS
        key = jax.random.key(seed)
        ks = jax.random.split(key, 11)
        B, S, E = (4, 256, EMBED)
        scale = 1.0 / np.sqrt(E)
        inp = {'Q': jax.random.normal(ks[0], (B, S, E), jnp.float32), 'K': jax.random.normal(ks[1], (B, S, E), jnp.float32), 'V': jax.random.normal(ks[2], (B, S, E), jnp.float32), 'Wq': jax.random.normal(ks[3], (E, E), jnp.float32) * scale, 'Wk': jax.random.normal(ks[4], (E, E), jnp.float32) * scale, 'Wv': jax.random.normal(ks[5], (E, E), jnp.float32) * scale, 'Wo': jax.random.normal(ks[6], (E, E), jnp.float32) * scale, 'bq': jax.random.normal(ks[7], (E,), jnp.float32) * 0.01, 'bk': jax.random.normal(ks[8], (E,), jnp.float32) * 0.01, 'bv': jax.random.normal(ks[9], (E,), jnp.float32) * 0.01, 'bo': jax.random.normal(ks[10], (E,), jnp.float32) * 0.01}
        return inp
    _L0_xattn_all = _L0_xattn_setup()
    _L0_xattn_in = {k: v for k, v in _L0_xattn_all.items() if k in ('Wq', 'Wk', 'Wv', 'Wo', 'bq', 'bk', 'bv', 'bo')}
    del _L0_xattn_all

    def _L0_ffn_setup():
        import jax, jax.numpy as jnp
        import numpy as np
        H_DIM, E_DIM = (128, 64)
        N_SHARED, N_ROUTED, TOP_K = (2, 16, 4)
        B, S = (4, 256)
        key = jax.random.key(seed)
        ks = jax.random.split(key, 6)
        sc = 1.0 / np.sqrt(H_DIM)
        ec = 1.0 / np.sqrt(E_DIM)
        return {'x': jax.random.normal(ks[0], (B, S, H_DIM), dtype=jnp.float32), 'shared_up': jax.random.uniform(ks[1], (N_SHARED, E_DIM, H_DIM), jnp.float32, -sc, sc), 'shared_down': jax.random.uniform(ks[2], (N_SHARED, H_DIM, E_DIM), jnp.float32, -ec, ec), 'routed_up': jax.random.uniform(ks[3], (N_ROUTED, E_DIM, H_DIM), jnp.float32, -sc, sc), 'routed_down': jax.random.uniform(ks[4], (N_ROUTED, H_DIM, E_DIM), jnp.float32, -ec, ec), 'router_w': jax.random.uniform(ks[5], (N_ROUTED, H_DIM), jnp.float32, -sc, sc)}
    _L0_ffn_all = _L0_ffn_setup()
    _L0_ffn_in = {k: v for k, v in _L0_ffn_all.items() if k in ('shared_up', 'shared_down', 'routed_up', 'routed_down', 'router_w')}
    del _L0_ffn_all
    return {'x': x, 'ctx_1024': ctx_1024, 'L0_xattn_Wq': _L0_xattn_in['Wq'], 'L0_xattn_Wk': _L0_xattn_in['Wk'], 'L0_xattn_Wv': _L0_xattn_in['Wv'], 'L0_xattn_Wo': _L0_xattn_in['Wo'], 'L0_xattn_bq': _L0_xattn_in['bq'], 'L0_xattn_bk': _L0_xattn_in['bk'], 'L0_xattn_bv': _L0_xattn_in['bv'], 'L0_xattn_bo': _L0_xattn_in['bo'], 'L0_ffn_shared_up': _L0_ffn_in['shared_up'], 'L0_ffn_shared_down': _L0_ffn_in['shared_down'], 'L0_ffn_routed_up': _L0_ffn_in['routed_up'], 'L0_ffn_routed_down': _L0_ffn_in['routed_down'], 'L0_ffn_router_w': _L0_ffn_in['router_w']}

def reference(x, ctx_1024, L0_xattn_Wq, L0_xattn_Wk, L0_xattn_Wv, L0_xattn_Wo, L0_xattn_bq, L0_xattn_bk, L0_xattn_bv, L0_xattn_bo, L0_ffn_shared_up, L0_ffn_shared_down, L0_ffn_routed_up, L0_ffn_routed_down, L0_ffn_router_w):
    import jax
    import jax.numpy as jnp

    def _L0_xattn_ref(Q, K, V, Wq, Wk, Wv, Wo, bq, bk, bv, bo):
        import jax, jax.numpy as jnp
        import numpy as np
        EMBED = 128
        HEADS = 16
        HEAD_DIM = EMBED // HEADS
        B, S, E = Q.shape
        H, Dh = (HEADS, HEAD_DIM)
        q = (Q @ Wq.T + bq).reshape(B, S, H, Dh).transpose(0, 2, 1, 3)
        k = (K @ Wk.T + bk).reshape(B, S, H, Dh).transpose(0, 2, 1, 3)
        v = (V @ Wv.T + bv).reshape(B, S, H, Dh).transpose(0, 2, 1, 3)
        A = jnp.einsum('bhqd,bhkd->bhqk', q, k) / np.sqrt(Dh).astype(np.float32)
        causal = jnp.tril(jnp.ones((S, S), dtype=bool))
        A = jnp.where(causal, A, -jnp.inf)
        w = jax.nn.softmax(A, axis=-1)
        out = jnp.einsum('bhqk,bhkd->bhqd', w, v)
        out = out.transpose(0, 2, 1, 3).reshape(B, S, E)
        return out @ Wo.T + bo

    def _L0_ffn_ref(x, shared_up, shared_down, routed_up, routed_down, router_w):
        import jax, jax.numpy as jnp
        import numpy as np
        H_DIM, E_DIM = (128, 64)
        N_SHARED, N_ROUTED, TOP_K = (2, 16, 4)
        B, S = (4, 256)
        b, s, h = x.shape
        xt = x.reshape(-1, h)
        up_s = jnp.einsum('th,seh->tse', xt, shared_up)
        shared = jnp.einsum('tse,she->th', jax.nn.gelu(up_s, approximate=False), shared_down)
        probs = jax.nn.softmax(xt @ router_w.T, axis=-1)
        topk_p, topk_i = jax.lax.top_k(probs, TOP_K)
        gate = jnp.zeros_like(probs).at[jnp.arange(xt.shape[0])[:, None], topk_i].add(topk_p)
        up_r = jnp.einsum('th,reh->tre', xt, routed_up)
        act = jax.nn.gelu(up_r, approximate=False) * gate[:, :, None]
        routed = jnp.einsum('tre,rhe->th', act, routed_down)
        return (shared + routed).reshape(b, s, h)
    x = x + _L0_xattn_ref(_layernorm(x, axis=-1), ctx_1024, ctx_1024, L0_xattn_Wq, L0_xattn_Wk, L0_xattn_Wv, L0_xattn_Wo, L0_xattn_bq, L0_xattn_bk, L0_xattn_bv, L0_xattn_bo)
    x = x + _L0_ffn_ref(_layernorm(x, axis=-1), L0_ffn_shared_up, L0_ffn_shared_down, L0_ffn_routed_up, L0_ffn_routed_down, L0_ffn_router_w)
    return x

_drawn_inputs = setup_inputs


def setup_inputs(seed=0):
    import zlib

    import numpy as np

    out = dict(_drawn_inputs(seed))
    spreads = {}
    factors = {'L0_xattn_bq': 23.384, 'L0_xattn_bk': 64.0, 'L0_xattn_bv': 5.672, 'L0_xattn_bo': 5.415}
    for name, (base, spread) in spreads.items():
        noise = np.random.default_rng([zlib.crc32(name.encode()), seed]).standard_normal(out[name].shape)
        drawn = base * np.exp(spread * noise) if base else spread * noise
        out[name] = jnp.asarray(drawn.astype(out[name].dtype))
    for name, factor in factors.items():
        out[name] = (out[name] * factor).astype(out[name].dtype)
    return out
```

```python
from contextlib import ExitStack

import numpy as np

import concourse.bass as bass
from concourse import mybir

F32 = mybir.dt.float32
F32R = mybir.dt.float32r
BF16 = mybir.dt.bfloat16
U32 = mybir.dt.uint32
ALU = mybir.AluOpType
ACT = mybir.ActivationFunctionType
AX = mybir.AxisListType.X

P = 128
BANK = 512


class Turn:

    def __init__(self, at, first, batches):
        self.at, self.first, self.batches = at, first, batches

    def batch(self, lag):
        c = self.at - lag
        return None if isinstance(c, int) and not 0 <= c < self.batches else c

    def side(self, lag):
        return (self.first - lag) % 2


def count(n):
    return max(n, 0) if isinstance(n, int) else n


def xattn_moe_kernel(nc, x, ctx_t, wq_t, wk_t, wv_t, wo_t, bq, bk, bv, bo, sup_t, rup_t, sdown, rdown, router_t,
                     ident, ident_bf, future, spread, expert_no, out):
    NB, S, E = x.shape
    T = NB * S
    H, DH = 16, 8
    QB = S // P
    G, J = 4, 4
    UNITS = 12
    NR, TOPK = router_t.shape[1], 4
    ED = 64
    NCH = (sup_t.shape[1] + rup_t.shape[1]) // P
    NTT = T // P
    NCT = T // BANK
    QROWS, MROWS, MROW0 = 3 * DH, 2, 96
    VW = 32
    LAST_LAG = 4
    QK_TICK = 3

    x_v = x.rearrange("b (t p) e -> p (b t) e", p=P)
    out_v = out.rearrange("b (t p) e -> p (b t) e", p=P)

    with ExitStack() as stack:
        def sb(name, shape, dt):
            return stack.enter_context(nc.sbuf_tensor("sb_" + name, shape, dt))

        def sem(name):
            return stack.enter_context(nc.semaphore("s_" + name))

        psum = stack.enter_context(nc.psum_tensor("psum", [P, 8, BANK], F32))
        BANK_M, BANK_S, BANK_PV, BANK_A, BANK_B = 0, 2, 4, 6, 7

        id_f = sb("id_f", [P, P], F32)
        id_b = sb("id_b", [P, P], BF16)
        fut = sb("fut", [P, P], BF16)
        spr = sb("spr", [3 * NR, NCH - 1, P], BF16)
        exno = sb("exno", [P, NR], F32)
        wq_sb = sb("wq", [E, P], F32)
        wk_sb = sb("wk", [E, P], F32)
        wv_sb = sb("wv", [E, P], F32)
        wo_sb = sb("wo", [P, E], F32)
        rw_sb = sb("rw", [E, NR], F32)
        bq_sb = sb("bq", [P, 1], F32)
        bk_sb = sb("bk", [P, 1], F32)
        bv_sb = sb("bv", [P, P], F32)
        bo_sb = sb("bo", [P, P], F32)
        up_h = sb("up_h", [E, NCH * P], F32R)
        up_l = sb("up_l", [E, NCH * P], F32R)
        dn_h = sb("dn_h", [P, NCH * E], F32R)
        dn_l = sb("dn_l", [P, NCH * E], F32R)
        ones = sb("ones", [MROWS * H, S], F32)

        x2 = sb("x2", [P, NTT, E], F32)
        xn = sb("xn", [P, NTT, E], F32)
        xn_t = sb("xn_t", [E, T], F32)
        st1 = sb("st1", [P, NTT, 6], F32)
        mv1 = sb("mv1", [P, NTT, 2], F32)
        var1 = sb("var1", [P, NTT], F32)
        rs1 = sb("rs1", [P, NTT], F32)
        halfs = sb("halfs", [P, NTT], F32)
        ctx2 = [sb(f"ctx{s}", [E, S], F32) for s in range(2)]

        qk = sb("qk", [P, 4, S], F32R)
        qk_op = [sb(f"qk_op{s}", [P, H, 2, S], F32R) for s in range(2)]
        q_op, k_op = [o[:, :, 0, :] for o in qk_op], [o[:, :, 1, :] for o in qk_op]
        v_op = [sb(f"v_op{s}", [P, QB, H, VW], F32) for s in range(2)]
        mx = [sb(f"mx{s}", [P, QB, H], F32) for s in range(2)]
        m_parts = [sb(f"m_parts{h}", [P, QB, MROWS, H // 2], F32R) for h in range(2)]
        m_t = [sb(f"m_t{h}", [MROWS * H // 2, S], F32R) for h in range(2)]
        probs = [sb(f"probs{g}", [P, J * S + J * P], F32) for g in range(G)]
        up_f, dn_f = probs[2][:, 0:NCH * P], probs[3][:, 0:NCH * E]
        o_raw = sb("o_raw", [P, G, S], F32)
        num = sb("num", [P, S], F32)
        den = sb("den", [P, S], F32)
        rden = sb("rden", [P, S], F32)
        att = sb("att", [P, S], F32)

        st2 = sb("st2", [P, QB, 6], F32)
        mv2 = sb("mv2", [P, QB, 2], F32)
        var2 = sb("var2", [P, QB], F32)
        rs2 = sb("rs2", [P, QB], F32)
        xn2 = sb("xn2", [P, QB, E], F32)
        xn2_t = sb("xn2_t", [E, S], F32)
        xh = sb("xh", [E, T], F32R)
        xl = sb("xl", [E, T], F32R)
        lg = sb("lg", [P, QB, NR], F32)
        top = sb("top", [P, QB, 8], F32)
        top_i = sb("top_i", [P, QB, 8], U32)
        lgm = sb("lgm", [P, QB, NR], F32)
        ex = sb("ex", [P, QB, NR], F32)
        exs = sb("exs", [P, QB], F32)
        rexs = sb("rexs", [P, QB], F32)
        is_top = sb("is_top", [P, QB, NR, TOPK], F32)
        chosen = sb("chosen", [P, QB, NR], F32)
        gsel = sb("gsel", [P, QB, NR], F32)
        gate = sb("gate", [P, QB, NR], F32)
        gres = [sb(f"gres{n}", [P, QB, NR], F32) for n in range(2)]
        g_parts = sb("g_parts", [P, QB, 3, NR], BF16)
        gate_t = sb("gate_t", [3 * NR, T], BF16)

        NF = 3
        gel = [probs[0][:, BANK * n:BANK * n + BANK] for n in range(NF)]
        hid = [probs[1][:, BANK * n:BANK * n + BANK] for n in range(NF)]
        hid_h = [sb(f"hid_h{n}", [P, BANK], F32R) for n in range(NF)]
        hid_l = [sb(f"hid_l{n}", [P, BANK], F32R) for n in range(NF)]
        y_t = o_raw[:, 0:2, :].rearrange("p g q -> p (g q)")
        y = o_raw[:, 2:4, :].rearrange("p g (a e) -> p (g a) e", e=E)

        x_in = [sem(f"x_in{q}") for q in range(4)]
        w_in, c_in, ff_in = sem("w_in"), sem("c_in"), sem("ff_in")
        zeros_set, ones_set, ones_in, half_set, v_ones_set = [sem(f"zeros_set{s}") for s in range(2)], sem("ones_set"), sem("ones_in"), sem("half_set"), sem("v_ones_set")
        stats1, rstd1, xn_done, xnt_ps, xnt_read = sem("stats1"), sem("rstd1"), sem("xn_done"), sem("xnt_ps"), sem("xnt_read")
        resid = sem("resid")
        w_hi, w_lo = sem("w_hi"), sem("w_lo")
        ctx_in = sem("ctx_in")
        qk_ps, qk_hi, qk_lo = sem("qk_ps"), sem("qk_hi"), sem("qk_lo")
        op_in = [sem(f"op_in{h}") for h in range(2)]
        v_ps, v_read = sem("v_ps"), sem("v_read")
        m_ps, m_max = sem("m_ps"), sem("m_max")
        m_split, mt_ps, mt_read = sem("m_split"), sem("mt_ps"), sem("mt_read")
        m_in = [sem(f"m_in{h}") for h in range(2)]
        s_ps, s_exp, s_mask = sem("s_ps"), sem("s_exp"), sem("s_mask")
        pv_ps, pv_read = sem("pv_ps"), sem("pv_read")
        num_in, den_in = sem("num_in"), sem("den_in")
        den_inv, att_done, o_ps, x2_done = sem("den_inv"), sem("att_done"), sem("o_ps"), sem("x2_done")
        stats2, rstd2, xn2_done = sem("stats2"), sem("rstd2"), sem("xn2_done")
        xn2t_ps, xn2t_read, xh_done, xl_done = sem("xn2t_ps"), sem("xn2t_read"), sem("xh_done"), sem("xl_done")
        r_ps, r_exp, r_step, g_last = sem("r_ps"), sem("r_exp"), sem("r_step"), sem("g_last")
        gt_ps, gt_read = sem("gt_ps"), sem("gt_read")
        u_ps, gate_ps, u_gelu, hid_done = sem("u_ps"), sem("gate_ps"), sem("u_gelu"), sem("hid_done")
        hid_hi, hid_lo, d_ps, d_read, y_ps, y_done = (sem("hid_hi"), sem("hid_lo"), sem("d_ps"), sem("d_read"),
                                                      sem("y_ps"), sem("y_done"))
        out_done, unused = sem("out_done"), sem("unused")
        RSTEPS = 15

        block = stack.enter_context(nc.Block())

        def apart(eng):
            eng.sem_inc(unused, 1)

        def attention(eng, turn_of):
            for i in range(LAST_LAG):
                turn_of(Turn(i, i, NB))
            with eng.Fori(0, (NB - LAST_LAG) // 2) as k:
                for u in range(2):
                    turn_of(Turn(k * 2 + (LAST_LAG + u), LAST_LAG + u, NB))
            for i in range(NB, NB + LAST_LAG):
                turn_of(Turn(i, i, NB))

        users = {
            BANK_A: [("qk", 0, qk_lo, 2, 2), ("router", 4, r_step, RSTEPS, 1), ("v", 1, v_read, 1, 1), ("gates", 4, gt_read, 1, 2)],
            BANK_B: [("max1", 2, mt_read, 2, 2), ("xn2", 4, xh_done, 1, 1), ("max0", 1, mt_read, 2, 1), ("o", 3, x2_done, 1, 1)],
        }

        def bank_free(turn, bank, step):
            order = users[bank]
            at = [u[0] for u in order].index(step)
            for back in range(1, 3 * len(order)):
                name, lag, reader, per, which = order[(at - back) % len(order)]
                c = Turn(turn.at - (0 if back <= at else 1 + (back - at - 1) // len(order)), 0, NB).batch(lag)
                if c is not None:
                    return reader, count(per * c + which)
            return None

        @block.sync
        def _(sp):
            for q in range(4):
                sp.dma_start(x2[:, 4 * q:4 * q + 4, :], x_v[:, 4 * q:4 * q + 4, :]).then_inc(x_in[q], 16)
                if q == 0:
                    for dst, src in ((wq_sb, wq_t), (wk_sb, wk_t)):
                        sp.dma_start(dst[:, :], src).then_inc(w_in, 16)
                    for dst, src in ((bq_sb, bq), (bk_sb, bk)):
                        sp.dma_start(dst[:, :], src).then_inc(w_in, 16)

            def operands(c, side, half):
                heads = slice(half * H // 2, (half + 1) * H // 2)
                rows = slice(half * P // 2, (half + 1) * P // 2)
                if isinstance(c, int) and c < 2:
                    sp.wait_ge(zeros_set[side], 2)
                sp.wait_ge(qk_lo, count(2 * c + 2))
                apart(sp)
                sp.wait_ge(s_ps, count(UNITS * (c - 2) + UNITS // 2 * (half + 1)))
                for n, pair in enumerate((qk[rows, 0:4:2, :], qk[rows, 0:4:3, :], qk[rows, 1:3, :])):
                    sp.dma_start(qk_op[side][DH * n:DH * n + DH, heads, :, :].bitcast(F32), pair.bitcast(F32)).then_inc(op_in[half], 16)

            def maxima(c, side, half):
                heads = slice(half * H // 2, (half + 1) * H // 2)
                sp.wait_ge(mt_read, count(2 * c + 1 + half))
                sp.dma_start(q_op[side][MROW0:MROW0 + MROWS, heads, :].bitcast(F32), m_t[half][:, :].bitcast(F32)).then_inc(m_in[half], 16)

            def turn_of(turn):
                c = turn.batch(0)
                if c is not None:
                    sp.wait_ge(v_ps, count(c - 1))
                    apart(sp)
                    start = c * S
                    sp.dma_start(ctx2[turn.side(0)][:, :], ctx_t[:, bass.ds(start, S)]).then_inc(ctx_in, 16)
                c = turn.batch(1)
                if c is not None:
                    operands(c, turn.side(1), 1)
                c = turn.batch(2)
                if c is not None:
                    maxima(c, turn.side(2), 1)
                c = turn.batch(3)
                if c is not None:
                    sp.wait_ge(pv_read, count(2 * c + 2))
                    sp.wait_ge(den_inv, count(c))
                    for j in range(J):
                        sp.dma_start(den[32 * j:32 * j + 32, :], o_raw[32 * j + DH:32 * j + 2 * DH, :, :]).then_inc(den_in, 16)
                    sp.wait_ge(att_done, count(c))
                    for j in range(J):
                        sp.dma_start(num[32 * j:32 * j + 32, :], o_raw[32 * j:32 * j + DH, :, :]).then_inc(num_in, 16)
                c = turn.batch(0)
                if c is not None:
                    operands(c, turn.side(0), 0)
                c = turn.batch(1)
                if c is not None:
                    maxima(c, turn.side(1), 0)

            attention(sp, turn_of)

            with sp.Fori(0, NCT) as n:
                sp.wait_ge(y_done, n + 2)
                apart(sp)
                sp.dma_start(out_v[:, bass.ds(n * (BANK // P), BANK // P), :], y).then_inc(out_done, 16)
            sp.wait_ge(out_done, 16 * (NCT + 1))

        @block.gpsimd
        def _(pool):
            nc.gpsimd.memset(halfs[:, :], -0.5).then_inc(half_set, 1)
            nc.gpsimd.memset(ones[:, :], 1.0).then_inc(ones_set, 1)
            def rstd_1(q):
                tiles = slice(4 * q, 4 * q + 4)
                pool.wait_ge(stats1, 8 * q + 8)
                nc.gpsimd.tensor_scalar(var1[:, tiles], mv1[:, tiles, 1], 1e-5, None, ALU.add).then_inc(rstd1, 1)
                pool.wait_ge(rstd1, 2 * q + 1)
                nc.gpsimd.tensor_tensor(rs1[:, tiles], var1[:, tiles], halfs[:, tiles], ALU.pow).then_inc(rstd1, 1)

            def lo_part(dst, full, high, n=slice(None)):
                return nc.gpsimd.tensor_tensor(dst[:, n], full[:, n], high[:, n].bitcast(F32), ALU.subtract)

            def select(c, t):
                g, u = divmod(t, 3)
                pool.wait_ge(s_exp, count(UNITS * c + t + 1))
                apart(pool)
                if u < 2:
                    v = probs[g][:, u * BANK:(u + 1) * BANK].rearrange("p (j q) -> p j q", j=2)[:, :, 0:P]
                else:
                    v = probs[g][:, J * S:J * S + J * P].rearrange("p (j q) -> p j q", j=J)
                nc.gpsimd.affine_select(out=v, in_=v, compare_op=ALU.is_ge, fill=0.0, base=0,
                                        pattern=[[0, v.shape[1]], [1, P]], channel_multiplier=-1).then_inc(s_mask, 1)

            def turn_of(turn):
                for t in range(UNITS):
                    c = turn.batch(4)
                    if t == 0 and c is not None:
                        pool.wait_ge(stats2, count(4 * c + 4))
                        apart(pool)
                        nc.gpsimd.tensor_scalar(var2[:, :], mv2[:, :, 1], 1e-5, None, ALU.add).then_inc(rstd2, 1)
                        pool.wait_ge(rstd2, count(2 * c + 1))
                        nc.gpsimd.tensor_tensor(rs2[:, :], var2[:, :], halfs[:, 0:QB], ALU.pow).then_inc(rstd2, 1)
                    c = turn.batch(2)
                    if c is not None:
                        select(c, t)
                    c = turn.batch(4)
                    if t == 6 and c is not None:
                        pool.wait_ge(xh_done, count(c + 1))
                        nc.gpsimd.tensor_tensor(xl[:, bass.ds(c * S, S)], xn2_t[:, :],
                                                xh[:, bass.ds(c * S, S)].bitcast(F32), ALU.subtract).then_inc(xl_done, 1)
                if not isinstance(turn.at, int):
                    return
                if turn.at == 0:
                    for q in range(1, 4):
                        rstd_1(q)
                    pool.wait_ge(xn_done, NTT)
                    pool.wait_ge(c_in, 16 * 9)
                    nc.gpsimd.tensor_tensor(x2[:, :, :], x2[:, :, :],
                                            bo_sb[:, :].unsqueeze(1).to_broadcast([P, NTT, E]), ALU.add).then_inc(resid, 1)
                if turn.at == 1:
                    pool.wait_ge(w_hi, 2)
                    lo_part(up_l, up_f, up_h).then_inc(w_lo, 1)
                    lo_part(dn_l, dn_f, dn_h).then_inc(w_lo, 1)

            pool.wait_ge(half_set, 1)
            nc.gpsimd.memset(qk_op[0][:, 0:H // 2, :, :].bitcast(F32), 0.0).then_inc(zeros_set[0], 1)
            rstd_1(0)
            nc.gpsimd.memset(qk_op[0][:, H // 2:H, :, :].bitcast(F32), 0.0).then_inc(zeros_set[0], 1)
            pool.wait_ge(ones_set, 1)
            for side in range(2):
                pool.wait_ge(zeros_set[side], 2)
                pool.dma_start(k_op[side][MROW0:MROW0 + MROWS, :, :].bitcast(F32), ones[:, :]).then_inc(ones_in, 16)
            for side in range(2):
                nc.gpsimd.memset(v_op[side][:, :, :, :], 1.0).then_inc(v_ones_set, 1)
            attention(pool, turn_of)

        @block.scalar
        def _(act):
            for dst, src in ((id_f, ident), (wv_sb, wv_t), (wo_sb, wo_t), (id_b, ident_bf), (fut, future),
                             (rw_sb, router_t), (exno, expert_no.partition_broadcast(P)),
                             (bv_sb, bv.partition_broadcast(P)), (bo_sb, bo.partition_broadcast(P))):
                act.dma_start(dst[:, :], src).then_inc(c_in, 16)
            act.sem_inc(gt_read, 1)
            act.dma_start(spr[:, :, :], spread).then_inc(ff_in, 16)
            act.dma_start(up_f[:, 0:P], sup_t).then_inc(ff_in, 16)
            act.dma_start(up_f[:, P:NCH * P], rup_t).then_inc(ff_in, 16)
            act.dma_start(dn_f[:, 0:E], sdown).then_inc(ff_in, 16)
            act.dma_start(dn_f[:, E:NCH * E].rearrange("p (c h) -> p c h", h=E), rdown).then_inc(ff_in, 16)

            def read_xn(q):
                act.wait_ge(xnt_ps, q + 1)
                nc.scalar.copy(xn_t[:, BANK * q:BANK * (q + 1)], psum[:, BANK_PV + q % 2, :]).then_inc(xnt_read, 1)

            def read_pv(c, n):
                act.wait_ge(pv_ps, count(G * c + 2 * n + 2))
                act.wait_ge(num_in, count(64 * c))
                act.wait_ge(den_in, count(64 * c))
                nc.scalar.copy(o_raw[:, 2 * n:2 * n + 2, :].rearrange("p g q -> p (g q)"), psum[:, BANK_PV + n, :])\
                    .then_inc(pv_read, 1)

            def read_maxima(c, half):
                act.wait_ge(mt_ps, count(2 * c + 1 + half))
                act.wait_ge(m_in[half], count(16 * c))
                nc.scalar.copy(m_t[half][:, :], psum[0:MROWS * H // 2, BANK_B, 0:S]).then_inc(mt_read, 1)

            def turn_of(turn):
                for t in range(UNITS):
                    c = turn.batch(2)
                    if c is not None:
                        g, u = divmod(t, 3)
                        act.wait_ge(s_ps, count(UNITS * c + t + 1))
                        nc.scalar.activation(probs[g][:, u * BANK:(u + 1) * BANK], psum[:, BANK_S + t % 2, :], ACT.Exp,
                                             scale=float(DH) ** -0.5).then_inc(s_exp, 1)
                    if t == 0 and c is not None:
                        read_maxima(c, 1)
                    c = turn.batch(0)
                    if t == QK_TICK and c is not None:
                        act.wait_ge(qk_ps, count(c + 1))
                        for half in range(2):
                            act.wait_ge(op_in[half], count(48 * c))
                        if isinstance(c, int) and c == 0:
                            act.wait_ge(w_in, 64)
                        for n, bias in enumerate((bq_sb, bk_sb)):
                            nc.scalar.activation(qk[:, 2 * n, :], psum[:, BANK_A, S * n:S * n + S], ACT.Identity,
                                                 bias=bias[:, :]).then_inc(qk_hi, 1)
                    c = turn.batch(3)
                    if t == 3 and c is not None:
                        read_pv(c, 1)
                    c = turn.batch(4)
                    if t == 3 and c is not None:
                        act.wait_ge(xn2t_ps, count(c + 1))
                        nc.scalar.copy(xn2_t[:, :], psum[:, BANK_B, 0:S]).then_inc(xn2t_read, 1)
                        nc.scalar.copy(xh[:, bass.ds(c * S, S)], psum[:, BANK_B, 0:S]).then_inc(xh_done, 1)
                    c = turn.batch(1)
                    if t == 7 and c is not None:
                        read_maxima(c, 0)
                    c = turn.batch(2)
                    if t == 9 and c is not None:
                        read_pv(c, 0)
                    c = turn.batch(4)
                    if t == 8 and c is not None:
                        act.wait_ge(r_step, count(RSTEPS * c + 6))
                        nc.scalar.activation(ex[:, :, :], lgm[:, :, :], ACT.Exp).then_inc(r_exp, 1)
                    if t == 11 and c is not None:
                        act.wait_ge(gt_ps, count(c + 1))
                        nc.scalar.copy(gate_t[:, bass.ds(c * S, S)], psum[0:3 * NR, BANK_A, 0:S // 2].bitcast(BF16))\
                            .then_inc(gt_read, 1)
                if not isinstance(turn.at, int):
                    return
                if turn.at == 0:
                    read_xn(1)
                if turn.at == 1:
                    read_xn(2)
                    read_xn(3)
                    act.wait_ge(ff_in, 16 * 5)
                    nc.scalar.copy(up_h[:, :], up_f).then_inc(w_hi, 1)
                    nc.scalar.copy(dn_h[:, :], dn_f).then_inc(w_hi, 1)
                    act.wait_ge(w_lo, 2)

            read_xn(0)
            attention(act, turn_of)

            def gelu(n, k):
                at = n * NCH + k
                act.wait_ge(u_ps, at + 1)
                act.wait_ge(hid_done, count(at - NF + 1) if isinstance(at, int) else at - NF + 1)
                nc.scalar.activation(gel[k % NF], psum[:, k % NF, :], ACT.Gelu).then_inc(u_gelu, 1)

            def high(n, k):
                at = n * NCH + k
                act.wait_ge(hid_done, at + 1)
                act.wait_ge(d_ps, count(at - NF + 1) if isinstance(at, int) else at - NF + 1)
                nc.scalar.copy(hid_h[k % NF][:, :], hid[k % NF]).then_inc(hid_hi, 1)

            def read_d(n):
                act.wait_ge(d_ps, (n + 1) * NCH)
                act.wait_ge(y_ps, n + 1)
                nc.scalar.copy(y_t, psum[:, 5, :]).then_inc(d_read, 1)

            def tile_of(n, first):
                for k in range(NCH):
                    gelu(n, k)
                    if k > 0:
                        high(n, k - 1)
                    elif not first:
                        high(n - 1, NCH - 1)
                    if k == 1 and not first:
                        read_d(n - 1)

            tile_of(0, True)
            with act.Fori(1, NCT) as n:
                tile_of(n, False)
            high(NCT - 1, NCH - 1)
            read_d(NCT - 1)

        @block.vector
        def _(dve):
            def stats_1(q):
                dve.wait_ge(x_in[q], 16)
                for a in range(4 * q, 4 * q + 4):
                    nc.vector.bn_stats(st1[:, a, :], x2[:, a, :]).then_inc(stats1, 1)
                for a in range(4 * q, 4 * q + 4):
                    dve.wait_ge(stats1, 8 * q + a % 4 + 1)
                    nc.vector.bn_aggr(mv1[:, a, :], st1[:, a, :]).then_inc(stats1, 1)
                dve.wait_ge(stats1, 8 * q + 8)

            def apply_1(q):
                dve.wait_ge(rstd1, 2 * q + 2)
                for a in range(4 * q, 4 * q + 4):
                    nc.vector.tensor_scalar(xn[:, a, :], x2[:, a, :], mv1[:, a, 0:1], rs1[:, a:a + 1],
                                            ALU.subtract, ALU.mult).then_inc(xn_done, 1)

            def split_maxima(c, side, half):
                heads = slice(half * H // 2, (half + 1) * H // 2)
                m = mx[side][:, :, heads]
                high, low = (m_parts[half][:, :, n, :] for n in range(2))
                dve.wait_ge(m_max, count(UNITS * c + UNITS // 2 * (half + 1)))
                dve.wait_ge(mt_ps, count(2 * c - 1 + half))
                nc.vector.tensor_scalar(high, m, -1.0, None, ALU.mult).then_inc(m_split, 1)
                dve.wait_ge(m_split, count(4 * c + 2 * half + 1))
                nc.vector.scalar_tensor_tensor(low, m, -1.0, high.bitcast(F32), ALU.mult, ALU.subtract).then_inc(m_split, 1)

            def choose(c):
                def step(n, ins):
                    ins.then_inc(r_step, 1)
                    return n + 1

                def after(n):
                    dve.wait_ge(r_step, count(RSTEPS * c + n))

                return step, after

            def turn_of(turn):
                for t in range(UNITS):
                    c = turn.batch(1)
                    if c is not None:
                        g, u = divmod(t, 3)
                        dve.wait_ge(m_ps, count(UNITS * c + t + 1))
                        if u < 2:
                            src = psum[:, BANK_M + t % 2, :].rearrange("p (j k) -> p j k", j=2)
                            dst = mx[turn.side(1)][:, 1, J * g + 2 * u:J * g + 2 * u + 2]
                        else:
                            src = psum[:, BANK_M + t % 2, :].rearrange("p (j k) -> p j k", j=J)
                            dst = mx[turn.side(1)][:, 0, J * g:J * g + J]
                        nc.vector.tensor_reduce(dst, src, AX, ALU.max).then_inc(m_max, 1)
                        if t in (5, 11):
                            split_maxima(c, turn.side(1), t // 6)
                    c = turn.batch(4)
                    if t == 1 and c is not None:
                        dve.wait_ge(rstd2, count(2 * c + 2))
                        for a in range(QB):
                            nc.vector.tensor_scalar(xn2[:, a, :], x2[:, bass.ds(c * QB + a, 1), :].rearrange("p a e -> p (a e)"),
                                                    mv2[:, a, 0:1], rs2[:, a:a + 1], ALU.subtract, ALU.mult)\
                                .then_inc(xn2_done, 1)
                    c = turn.batch(0)
                    if t == QK_TICK + 1 and c is not None:
                        dve.wait_ge(qk_hi, count(2 * c + 2))
                        for n, bias in enumerate((bq_sb, bk_sb)):
                            nc.vector.scalar_tensor_tensor(qk[:, 2 * n + 1, :], psum[:, BANK_A, S * n:S * n + S], bias[:, :],
                                                           qk[:, 2 * n, :].bitcast(F32), ALU.add, ALU.subtract).then_inc(qk_lo, 1)
                    c = turn.batch(4)
                    if t == 6 and c is not None:
                        step, after = choose(c)
                        dve.wait_ge(r_ps, count(c + 1))
                        n = step(0, nc.vector.tensor_copy(lg[:, :, :].rearrange("p a r -> p (a r)"), psum[:, BANK_A, 0:QB * NR]))
                        after(n)
                        apart(dve)
                        for a in range(QB):
                            n = step(n, nc.vector.max(top[:, a, :], lg[:, a, :]))
                        after(n)
                        apart(dve)
                        for a in range(QB):
                            n = step(n, nc.vector.max_index(top_i[:, a, :], top[:, a, :], lg[:, a, :]))
                        n = step(n, nc.vector.tensor_tensor(lgm[:, :, :], lg[:, :, :],
                                                            top[:, :, 0:1].to_broadcast([P, QB, NR]), ALU.subtract))
                        after(n)
                        n = step(n, nc.vector.tensor_tensor(
                            is_top[:, :, :, :], exno[:, :].unsqueeze(1).unsqueeze(3).to_broadcast([P, QB, NR, TOPK]),
                            top_i[:, :, 0:TOPK].unsqueeze(2).to_broadcast([P, QB, NR, TOPK]), ALU.is_equal))
                        after(n)
                        n = step(n, nc.vector.tensor_reduce(chosen[:, :, :], is_top[:, :, :, :], AX, ALU.add))
                    if t == 9 and c is not None:
                        step, after = choose(c)
                        n = 8
                        dve.wait_ge(r_exp, count(c + 1))
                        n = step(n, nc.vector.tensor_reduce(exs[:, :], ex[:, :, :], AX, ALU.add))
                        after(n)
                        n = step(n, nc.vector.reciprocal(rexs[:, :], exs[:, :]))
                        n = step(n, nc.vector.tensor_tensor(gsel[:, :, :], ex[:, :, :], chosen[:, :, :], ALU.mult))
                        after(n)
                        n = step(n, nc.vector.tensor_tensor(gate[:, :, :], gsel[:, :, :],
                                                            rexs[:, :].unsqueeze(2).to_broadcast([P, QB, NR]), ALU.mult))
                        after(n)
                        n = step(n, nc.vector.tensor_copy(g_parts[:, :, 0, :], gate[:, :, :]))
                        after(n)
                        n = step(n, nc.vector.tensor_tensor(gres[0][:, :, :], gate[:, :, :], g_parts[:, :, 0, :], ALU.subtract))
                        after(n)
                        n = step(n, nc.vector.tensor_copy(g_parts[:, :, 1, :], gres[0][:, :, :]))
                        after(n)
                        nc.vector.tensor_tensor(g_parts[:, :, 2, :], gres[0][:, :, :], g_parts[:, :, 1, :], ALU.subtract)\
                            .then_inc(g_last, 1)
                        assert n == RSTEPS
                    c = turn.batch(3)
                    if t == 8 and c is not None:
                        dve.wait_ge(den_in, count(64 * (c + 1)))
                        nc.vector.reciprocal(rden[:, :], den[:, :]).then_inc(den_inv, 1)
                        dve.wait_ge(den_inv, count(c + 1))
                        dve.wait_ge(num_in, count(64 * (c + 1)))
                        dve.wait_ge(o_ps, count(c))
                        nc.vector.tensor_tensor(att[:, :], num[:, :], rden[:, :], ALU.mult).then_inc(att_done, 1)
                    c = turn.batch(1)
                    if t == 10 and c is not None:
                        dve.wait_ge(v_ps, count(c + 1))
                        dve.wait_ge(pv_ps, count(G * (c - 1)))
                        if isinstance(c, int) and c == 0:
                            dve.wait_ge(v_ones_set, 2)
                            dve.wait_ge(c_in, 16 * 9)
                        nc.vector.tensor_tensor(
                            v_op[turn.side(1)][:, :, :, 0:DH],
                            psum[:, BANK_A, 0:QB * P].rearrange("p (a h d) -> p a h d", a=QB, h=H),
                            bv_sb[:, :].rearrange("p (h d) -> p h d", h=H).unsqueeze(1).to_broadcast([P, QB, H, DH]),
                            ALU.add).then_inc(v_read, 1)
                    c = turn.batch(3)
                    if t == 11 and c is not None:
                        dve.wait_ge(o_ps, count(c + 1))
                        dve.wait_ge(resid, 1)
                        rows = x2[:, bass.ds(c * QB, QB), :]
                        nc.vector.tensor_tensor(rows, psum[:, BANK_B, 0:QB * P].rearrange("p (a e) -> p a e", a=QB), rows,
                                                ALU.add).then_inc(x2_done, 1)
                        dve.wait_ge(x2_done, count(c + 1))
                        dve.wait_ge(rstd2, count(2 * c))
                        apart(dve)
                        for a in range(QB):
                            nc.vector.bn_stats(st2[:, a, :], x2[:, bass.ds(c * QB + a, 1), :].rearrange("p a e -> p (a e)"))\
                                .then_inc(stats2, 1)
                        for a in range(QB):
                            dve.wait_ge(stats2, count(4 * c + a + 1))
                            apart(dve)
                            nc.vector.bn_aggr(mv2[:, a, :], st2[:, a, :]).then_inc(stats2, 1)
                if isinstance(turn.at, int) and turn.at == 0:
                    for q in range(1, 4):
                        stats_1(q)
                        apply_1(q)

            stats_1(0)
            apply_1(0)
            for half in range(2):
                nc.vector.memset(qk_op[1][:, half * H // 2:(half + 1) * H // 2, :, :].bitcast(F32), 0.0).then_inc(zeros_set[1], 1)
            attention(dve, turn_of)

            def gated(n, k):
                at = n * NCH + k
                dve.wait_ge(u_gelu, at + 1)
                dve.wait_ge(hid_lo, count(at - NF + 1) if isinstance(at, int) else at - NF + 1)
                if k == 0:
                    nc.vector.tensor_copy(hid[k % NF], gel[k % NF]).then_inc(hid_done, 1)
                else:
                    dve.wait_ge(gate_ps, (NCH - 1) * n + k)
                    nc.vector.tensor_tensor(hid[k % NF], gel[k % NF], psum[:, 3 + k % 2, :], ALU.mult)\
                        .then_inc(hid_done, 1)

            def low(n, k):
                at = n * NCH + k
                dve.wait_ge(hid_hi, at + 1)
                dve.wait_ge(d_ps, count(at - NF + 1) if isinstance(at, int) else at - NF + 1)
                nc.vector.tensor_tensor(hid_l[k % NF][:, :], hid[k % NF], hid_h[k % NF][:, :].bitcast(F32),
                                        ALU.subtract).then_inc(hid_lo, 1)

            def finish(n):
                dve.wait_ge(y_ps, n + 2)
                dve.wait_ge(out_done, 16 * (n + 1))
                nc.vector.tensor_tensor(y, psum[:, 6, :].rearrange("p (a e) -> p a e", e=E),
                                        x2[:, bass.ds(n * (BANK // P), BANK // P), :], ALU.add).then_inc(y_done, 1)

            def tile_of(n, first):
                for k in range(NCH):
                    gated(n, k)
                    if k > 0:
                        low(n, k - 1)
                    elif not first:
                        low(n - 1, NCH - 1)
                    if k == 3 and not first:
                        finish(n - 1)

            tile_of(0, True)
            with dve.Fori(1, NCT) as n:
                tile_of(n, False)
            low(NCT - 1, NCH - 1)
            finish(NCT - 1)

        @block.tensor
        def _(pe):
            mm = nc.tensor.matmul

            def wait_bank(turn, bank, step):
                got = bank_free(turn, bank, step)
                if got is not None:
                    pe.wait_ge(*got)

            def transpose_xn(q):
                pe.wait_ge(xn_done, 4 * q + 4)
                if q >= 2:
                    pe.wait_ge(xnt_read, q - 1)
                for a in range(4):
                    last = nc.tensor.transpose(psum[:, BANK_PV + q % 2, P * a:P * a + P], xn[:, 4 * q + a, :], id_f[:, :])
                last.then_inc(xnt_ps, 1)

            def max_unit(c, side, t):
                g, u = divmod(t, 3)
                if t % 6 == 0:
                    pe.wait_ge(op_in[t // 6], count(48 * (c + 1)))
                pe.wait_ge(m_max, count(UNITS * c + t - 1))
                bank = psum[:, BANK_M + t % 2, :]
                if u < 2:
                    heads = [J * g + 2 * u, J * g + 2 * u + 1]
                    v = bank.rearrange("p (j k) -> p j k", j=2)
                    mm(v[:, :, P:2 * P], id_b[:, :], fut[:, :].unsqueeze(1).to_broadcast([P, 2, P]), start=True, stop=False,
                       skip_group_check=True)
                    for n, h in enumerate(heads):
                        last = mm(v[:, n, :], q_op[side][0:MROW0, h, P:2 * P], k_op[side][0:MROW0, h, :], start=False,
                                  stop=(n == 1), skip_group_check=True)
                else:
                    v = bank.rearrange("p (j k) -> p j k", j=J)
                    mm(v, id_b[:, :], fut[:, :].unsqueeze(1).to_broadcast([P, J, P]), start=True, stop=False,
                       skip_group_check=True)
                    for n in range(J):
                        last = mm(v[:, n, :], q_op[side][0:MROW0, J * g + n, 0:P], k_op[side][0:MROW0, J * g + n, 0:P],
                                  start=False, stop=(n == J - 1), skip_group_check=True)
                last.then_inc(m_ps, 1)

            def exp_unit(c, side, t):
                g, u = divmod(t, 3)
                if t % 6 == 0:
                    pe.wait_ge(m_in[t // 6], count(16 * (c + 1)))
                pe.wait_ge(s_exp, count(UNITS * c + t - 1))
                bank = psum[:, BANK_S + t % 2, :]
                if u < 2:
                    for n in range(2):
                        h = J * g + 2 * u + n
                        last = mm(bank[:, S * n:S * n + S], k_op[side][:, h, 0:P], q_op[side][:, h, :], start=True, stop=True)
                else:
                    for n in range(J):
                        h = J * g + n
                        last = mm(bank[:, P * n:P * n + P], k_op[side][:, h, P:2 * P], q_op[side][:, h, P:2 * P],
                                  start=True, stop=True)
                last.then_inc(s_ps, 1)

            def pv(c, side, g):
                pe.wait_ge(s_mask, count(UNITS * c + 3 * g + 3))
                if g == 0:
                    pe.wait_ge(v_read, count(c + 1))
                if g % 2 == 0:
                    pe.wait_ge(pv_read, count(2 * c - 1 + g // 2))
                col = S * (g % 2)
                bank = psum[:, BANK_PV + g // 2, :]
                for j in range(J):
                    mm(bank[32 * j:32 * j + 32, col:col + S], v_op[side][:, 0, J * g + j, :],
                       probs[g][:, S * j:S * j + S], start=True, stop=False)
                for j in range(J):
                    last = mm(bank[32 * j:32 * j + 32, col + P:col + S], v_op[side][:, 1, J * g + j, :],
                              probs[g][:, J * S + P * j:J * S + P * j + P], start=False, stop=True)
                last.then_inc(pv_ps, 1)

            def transpose_maxima(turn, c, half):
                pe.wait_ge(m_split, count(4 * c + 2 * half + 2))
                wait_bank(turn, BANK_B, f"max{half}")
                apart(pe)
                for a in range(QB):
                    last = nc.tensor.transpose(psum[0:MROWS * H // 2, BANK_B, P * a:P * a + P],
                                               m_parts[half][:, a, :, :].rearrange("p m h -> p (m h)").bitcast(F32), id_f[:, :])
                last.then_inc(mt_ps, 1)

            def turn_of(turn):
                for t in range(UNITS):
                    c = turn.batch(1)
                    if c is not None:
                        max_unit(c, turn.side(1), t)
                    c = turn.batch(2)
                    if c is not None:
                        exp_unit(c, turn.side(2), t)
                        if t in (5, 8, 11):
                            pv(c, turn.side(2), (t - 5) // 3)
                        if t == 0:
                            transpose_maxima(turn, c, 1)
                    c = turn.batch(3)
                    if t == 2 and c is not None:
                        pv(c, turn.side(3), 3)
                    c = turn.batch(0)
                    if t == QK_TICK and c is not None:
                        pe.wait_ge(ctx_in, count(16 * (c + 1)))
                        if isinstance(c, int) and c % 2 == 0:
                            pe.wait_ge(xnt_read, c // 2 + 1)
                        wait_bank(turn, BANK_A, "qk")
                        mm(psum[:, BANK_A, 0:S], wq_sb[:, :], xn_t[:, bass.ds(c * S, S)], start=True, stop=True)
                        mm(psum[:, BANK_A, S:2 * S], wk_sb[:, :], ctx2[turn.side(0)][:, :], start=True, stop=True)\
                            .then_inc(qk_ps, 1)
                    c = turn.batch(4)
                    if t == 3 and c is not None:
                        pe.wait_ge(xn2_done, count(QB * (c + 1)))
                        wait_bank(turn, BANK_B, "xn2")
                        for a in range(QB):
                            last = nc.tensor.transpose(psum[:, BANK_B, P * a:P * a + P], xn2[:, a, :], id_f[:, :])
                        last.then_inc(xn2t_ps, 1)
                    if t == 5 and c is not None:
                        pe.wait_ge(xn2t_read, count(c + 1))
                        wait_bank(turn, BANK_A, "router")
                        for a in range(QB):
                            last = mm(psum[:, BANK_A, NR * a:NR * a + NR], xn2_t[:, P * a:P * a + P], rw_sb[:, :],
                                      start=True, stop=True)
                        last.then_inc(r_ps, 1)
                    c = turn.batch(1)
                    if t == 7 and c is not None:
                        transpose_maxima(turn, c, 0)
                    if t == 9 and c is not None:
                        wait_bank(turn, BANK_A, "v")
                        for a in range(QB):
                            last = mm(psum[:, BANK_A, P * a:P * a + P], ctx2[turn.side(1)][:, P * a:P * a + P], wv_sb[:, :],
                                      start=True, stop=True)
                        last.then_inc(v_ps, 1)
                    c = turn.batch(3)
                    if t == 10 and c is not None:
                        pe.wait_ge(att_done, count(c + 1))
                        wait_bank(turn, BANK_B, "o")
                        for a in range(QB):
                            last = mm(psum[:, BANK_B, P * a:P * a + P], att[:, P * a:P * a + P], wo_sb[:, :],
                                      start=True, stop=True)
                        last.then_inc(o_ps, 1)
                    c = turn.batch(4)
                    if t == 11 and c is not None:
                        pe.wait_ge(g_last, count(c + 1))
                        wait_bank(turn, BANK_A, "gates")
                        apart(pe)
                        bank = psum[:, BANK_A, :].bitcast(BF16)
                        for a in range(QB):
                            last = nc.tensor.transpose(bank[0:3 * NR, P * a:P * a + P],
                                                       g_parts[:, a, :, :].rearrange("p n r -> p (n r)"), id_b[:, :])
                        last.then_inc(gt_ps, 1)
                if not isinstance(turn.at, int):
                    return
                if turn.at == 0:
                    transpose_xn(1)
                    pe.wait_ge(ones_in, 32)
                if turn.at == 1:
                    transpose_xn(2)
                    transpose_xn(3)
                    pe.wait_ge(xnt_read, 4)

            pe.wait_ge(c_in, 16 * 9)
            transpose_xn(0)
            pe.wait_ge(w_in, 64)
            attention(pe, turn_of)

            pe.sem_inc(y_ps, 1)
            pe.sem_inc(y_done, 1)
            pe.sem_inc(out_done, 16)
            pe.wait_ge(w_lo, 2)
            pe.wait_ge(ff_in, 80)
            pe.wait_ge(xl_done, NB)
            pe.wait_ge(gt_read, NB + 1)

            def up(n, k):
                at = n * NCH + k
                cols = bass.ds(n * BANK, BANK)
                w = slice(P * k, P * k + P)
                pe.wait_ge(u_gelu, count(at - NF + 1) if isinstance(at, int) else at - NF + 1)
                mm(psum[:, k % NF, :], up_h[:, w], xh[:, cols], start=True, stop=False)
                mm(psum[:, k % NF, :], up_h[:, w], xl[:, cols], start=False, stop=False)
                mm(psum[:, k % NF, :], up_l[:, w], xh[:, cols], start=False, stop=True).then_inc(u_ps, 1)
                if k > 0:
                    pe.wait_ge(hid_done, count(at - 1) if isinstance(at, int) else at - 1)
                    apart(pe)
                    mm(psum[:, 3 + k % 2, :], spr[:, k - 1, :], gate_t[:, cols], start=True, stop=True).then_inc(gate_ps, 1)

            def down(n, k):
                at = n * NCH + k
                w = slice(E * k, E * k + E)
                if k == 0:
                    pe.wait_ge(d_read, n)
                pe.wait_ge(hid_hi, at + 1)
                mm(psum[:, 5, :], dn_h[:, w], hid_h[k % NF][:, :], start=(k == 0), stop=False)
                mm(psum[:, 5, :], dn_l[:, w], hid_h[k % NF][:, :], start=False, stop=False)
                pe.wait_ge(hid_lo, at + 1)
                mm(psum[:, 5, :], dn_h[:, w], hid_l[k % NF][:, :], start=False, stop=(k == NCH - 1)).then_inc(d_ps, 1)

            def transpose_y(n):
                pe.wait_ge(d_read, n + 1)
                pe.wait_ge(y_done, n + 1)
                for a in range(BANK // P):
                    last = nc.tensor.transpose(psum[:, 6, P * a:P * a + P], y_t[:, P * a:P * a + P], id_f[:, :])
                last.then_inc(y_ps, 1)

            def tile_of(n, first):
                for k in range(NCH):
                    up(n, k)
                    if k >= 2:
                        down(n, k - 2)
                    elif not first:
                        down(n - 1, NCH - 2 + k)
                    if k == 2 and not first:
                        transpose_y(n - 1)

            tile_of(0, True)
            with pe.Fori(1, NCT) as n:
                tile_of(n, False)
            down(NCT - 1, NCH - 2)
            down(NCT - 1, NCH - 1)
            transpose_y(NCT - 1)


def kernel(x, ctx_1024, L0_xattn_Wq, L0_xattn_Wk, L0_xattn_Wv, L0_xattn_Wo, L0_xattn_bq, L0_xattn_bk, L0_xattn_bv,
           L0_xattn_bo, L0_ffn_shared_up, L0_ffn_shared_down, L0_ffn_routed_up, L0_ffn_routed_down, L0_ffn_router_w):
    import concourse.bacc as bacc
    import ml_dtypes
    from concourse.bass_utils import run_bass_kernel_spmd

    nb, s, e = x.shape
    heads, dh = 16, 8
    n = np.arange(e).reshape(2, heads // 2, dh).transpose(0, 2, 1).reshape(-1)
    r = np.arange(e).reshape(4, 4, dh).transpose(1, 2, 0).reshape(-1)
    n_routed, ed, _ = L0_ffn_routed_up.shape
    n_shared = L0_ffn_shared_up.shape[0]
    pairs = n_routed // 2
    spread = np.zeros((3, n_routed, pairs, 128), np.float32)
    for c in range(pairs):
        for half in range(2):
            spread[:, 2 * c + half, c, ed * half:ed * half + ed] = 1.0
    future = np.where(np.arange(128)[None, :] > np.arange(128)[:, None], -1e30, 0.0)
    arrays = {
        "x": x,
        "ctx_t": np.asarray(ctx_1024).reshape(nb * s, e).T,
        "wq_t": np.asarray(L0_xattn_Wq)[n].T,
        "wk_t": np.asarray(L0_xattn_Wk)[n].T,
        "wv_t": np.asarray(L0_xattn_Wv).T,
        "wo_t": np.asarray(L0_xattn_Wo)[:, r].T,
        "bq": np.asarray(L0_xattn_bq)[n][:, None],
        "bk": np.asarray(L0_xattn_bk)[n][:, None],
        "bv": L0_xattn_bv,
        "bo": L0_xattn_bo,
        "sup_t": np.asarray(L0_ffn_shared_up).reshape(n_shared * ed, e).T,
        "rup_t": np.asarray(L0_ffn_routed_up).reshape(n_routed * ed, e).T,
        "sdown": np.asarray(L0_ffn_shared_down).transpose(0, 2, 1).reshape(n_shared * ed, e),
        "rdown": np.asarray(L0_ffn_routed_down).transpose(0, 2, 1).reshape(pairs, 128, e).transpose(1, 0, 2),
        "router_t": np.asarray(L0_ffn_router_w).T,
        "ident": np.eye(128, dtype=np.float32),
        "ident_bf": np.eye(128).astype(ml_dtypes.bfloat16),
        "future": future.astype(ml_dtypes.bfloat16),
        "spread": spread.reshape(3 * n_routed, pairs, 128).astype(ml_dtypes.bfloat16),
        "expert_no": np.arange(n_routed, dtype=np.float32),
    }
    nc = bacc.Bacc("TRN2", target_bir_lowering=False, num_devices=1)
    given, args = {}, []
    for name, a in arrays.items():
        a = np.ascontiguousarray(a)
        given[f"in_{name}"] = a
        args.append(nc.dram_tensor(f"in_{name}", a.shape, mybir.dt.from_np(a.dtype), kind="ExternalInput").ap())
    args.append(nc.dram_tensor("out_0", (nb, s, e), mybir.dt.float32, kind="ExternalOutput").ap())
    xattn_moe_kernel(nc, *args)
    got = run_bass_kernel_spmd(nc, [given], core_ids=[0])
    return got.results[0]["out_0"]
```

```python
from contextlib import ExitStack

import numpy as np

import concourse.bass as bass
from concourse import mybir

F32 = mybir.dt.float32
F32R = mybir.dt.float32r
BF16 = mybir.dt.bfloat16
U32 = mybir.dt.uint32
ALU = mybir.AluOpType
ACT = mybir.ActivationFunctionType
AX = mybir.AxisListType.X

P = 128
BANK = 512


class Turn:

    def __init__(self, at, first, batches):
        self.at, self.first, self.batches = at, first, batches

    def batch(self, lag):
        c = self.at - lag
        return None if isinstance(c, int) and not 0 <= c < self.batches else c

    def side(self, lag):
        return (self.first - lag) % 2


def count(n):
    return max(n, 0) if isinstance(n, int) else n


def xattn_moe_kernel(nc, x, ctx_t, wq_t, wk_t, wv_t, wo_t, bq, bk, bv, bo, sup_t, rup_t, sdown, rdown, router_t,
                     ident, ident_bf, future, spread, expert_no, head_rows, out):
    NB, S, E = x.shape
    T = NB * S
    H, DH = 16, 8
    QB = S // P
    G, J = 4, 4
    UNITS = 12
    NR, TOPK = router_t.shape[1], 4
    ED = 64
    NCH = (sup_t.shape[1] + rup_t.shape[1]) // P
    NTT = T // P
    NCT = T // BANK
    PAIRS = ((0, 3), (0, 4), (0, 5), (1, 3), (1, 4), (2, 3))
    MROWS, MROW0 = 2, 96
    VW = 32
    VSTEP = VW // DH
    LAST_LAG = 4
    QK_TICK = 1

    x_v = x.rearrange("b (t p) e -> p (b t) e", p=P)
    out_v = out.rearrange("b (t p) e -> p (b t) e", p=P)

    with ExitStack() as stack:
        def sb(name, shape, dt):
            return stack.enter_context(nc.sbuf_tensor("sb_" + name, shape, dt))

        def sem(name):
            return stack.enter_context(nc.semaphore("s_" + name))

        psum = stack.enter_context(nc.psum_tensor("psum", [P, 8, BANK], F32))
        BANK_M, MB, BANK_S, SB, BANK_PV, BANK_A, BANK_B = 0, 3, 3, 2, 5, 6, 7

        id_f = sb("id_f", [P, P], F32)
        id_b = sb("id_b", [P, P], BF16)
        fut = sb("fut", [P, P], BF16)
        spr = sb("spr", [3 * NR, NCH - 1, P], BF16)
        hrow = sb("hrow", [H, P], F32)
        exno = sb("exno", [P, NR], F32)
        wq_sb = sb("wq", [E, P], F32)
        wk_sb = sb("wk", [E, P], F32)
        wv_sb = sb("wv", [E, P], F32)
        wo_sb = sb("wo", [P, E], F32)
        rw_sb = sb("rw", [E, NR], F32)
        bq_sb = sb("bq", [P, 1], F32)
        bk_sb = sb("bk", [P, 1], F32)
        bv_sb = sb("bv", [1, P], F32)
        bo_sb = sb("bo", [P, P], F32)
        up_h = sb("up_h", [E, NCH * P], F32R)
        up_l = sb("up_l", [E, NCH * P], F32R)
        dn_h = sb("dn_h", [P, NCH * E], F32R)
        dn_l = sb("dn_l", [P, NCH * E], F32R)
        zero = sb("zero", [P, 1], F32)
        first_exp = sb("first_exp", [P, 1], F32)
        ones = sb("ones", [1, P], F32)
        ones_b = sb("ones_b", [MROWS * H, S], BF16)

        x2 = sb("x2", [P, NTT, E], F32)
        xn = sb("xn", [P, NTT, E], F32)
        xn_t = sb("xn_t", [E, T], F32)
        st1 = sb("st1", [P, NTT, 6], F32)
        mv1 = sb("mv1", [P, NTT, 2], F32)
        var1 = sb("var1", [P, NTT], F32)
        rs1 = sb("rs1", [P, NTT], F32)
        halfs = sb("halfs", [P, NTT], F32)
        ctx2 = [sb(f"ctx{s}", [E, S], F32) for s in range(2)]

        qk2 = [sb(f"qk{s}", [P, 6, S], BF16) for s in range(2)]
        qk_res = sb("qk_res", [P, 2, S], F32)
        qk_op = [sb(f"qk_op{s}", [P, H, 2, S], BF16) for s in range(2)]
        q_op, k_op = [o[:, :, 0, :] for o in qk_op], [o[:, :, 1, :] for o in qk_op]
        v_op = [sb(f"v_op{s}", [P, QB, H, VW], F32) for s in range(2)]
        mx = [sb(f"mx{s}", [P, QB, H], F32) for s in range(2)]
        m_parts = [sb(f"m_parts{h}", [P, QB, MROWS, H // 2], BF16) for h in range(2)]
        m_t = [sb(f"m_t{h}", [MROWS * H // 2, S], BF16) for h in range(2)]
        probs = [sb(f"probs{g}", [P, J * S + J * P], F32) for g in range(G)]
        up_f, dn_f = probs[2][:, 0:NCH * P], probs[3][:, 0:NCH * E]
        o_raw = sb("o_raw", [P, G, S], F32)
        num = sb("num", [P, S], F32)
        den = sb("den", [P, H * S // P], F32)
        rden = sb("rden", [P, H * S // P], F32)
        rden_h = sb("rden_h", [H, S], F32)
        att = sb("att", [P, S], F32)

        st2 = sb("st2", [P, QB, 6], F32)
        mv2 = sb("mv2", [P, QB, 2], F32)
        var2 = sb("var2", [P, QB], F32)
        rs2 = sb("rs2", [P, QB], F32)
        xn2 = sb("xn2", [P, QB, E], F32)
        xn2_t = sb("xn2_t", [E, S], F32)
        xh = sb("xh", [E, T], F32R)
        xl = sb("xl", [E, T], F32R)
        top = sb("top", [P, QB, 8], F32)
        top_i = sb("top_i", [P, QB, 8], U32)
        lgm = sb("lgm", [P, QB, NR], F32)
        ex = sb("ex", [P, QB, NR], F32)
        exs = sb("exs", [P, QB], F32)
        rexs = sb("rexs", [P, QB], F32)
        is_top = sb("is_top", [P, QB, NR, TOPK], F32)
        chosen = sb("chosen", [P, QB, NR], F32)
        gsel = sb("gsel", [P, QB, NR], F32)
        gate = sb("gate", [P, QB, NR], F32)
        gres = sb("gres", [P, QB, NR], F32)
        g_parts = sb("g_parts", [P, QB, 3, NR], BF16)
        gate_t = sb("gate_t", [3 * NR, T], BF16)

        NF = 3
        gel = [probs[0][:, BANK * n:BANK * n + BANK] for n in range(NF)]
        hid = [probs[1][:, BANK * n:BANK * n + BANK] for n in range(NF)]
        hid_h = [sb(f"hid_h{n}", [P, BANK], F32R) for n in range(NF)]
        hid_l = [sb(f"hid_l{n}", [P, BANK], F32R) for n in range(NF)]
        y_t = o_raw[:, 0:2, :].rearrange("p g q -> p (g q)")
        y = o_raw[:, 2:4, :].rearrange("p g (a e) -> p (g a) e", e=E)

        x_in = [sem(f"x_in{q}") for q in range(4)]
        id_in, w_in, c_in, ff_in = sem("id_in"), sem("w_in"), sem("c_in"), sem("ff_in")
        zero_set, half_set, ones_set, ones_in, v_ones_set = (sem("zero_set"), sem("half_set"), sem("ones_set"),
                                                             sem("ones_in"), sem("v_ones_set"))
        zeros_set = [sem(f"zeros_set{s}") for s in range(2)]
        stats1, rstd1, xn_done, xnt_ps, xnt_read = sem("stats1"), sem("rstd1"), sem("xn_done"), sem("xnt_ps"), sem("xnt_read")
        resid = sem("resid")
        w_hi, w_lo = sem("w_hi"), sem("w_lo")
        ctx_in, ctx1_in = sem("ctx_in"), sem("ctx1_in")
        qk_ps, qk_hi, qk_less = sem("qk_ps"), sem("qk_hi"), sem("qk_less")
        qk_mid, qk_lo = sem("qk_mid"), sem("qk_lo")
        op_in = [sem(f"op_in{h}") for h in range(2)]
        v_ps, v_read = sem("v_ps"), sem("v_read")
        m_ps, m_max = sem("m_ps"), sem("m_max")
        m_split, mt_ps, mt_read = sem("m_split"), sem("mt_ps"), sem("mt_read")
        m_in = [sem(f"m_in{h}") for h in range(2)]
        s_ps, s_exp, s_mask = sem("s_ps"), sem("s_exp"), sem("s_mask")
        pv_ps, pv_read = sem("pv_ps"), sem("pv_read")
        num_in, den_in, rden_in = sem("num_in"), sem("den_in"), sem("rden_in")
        den_inv, rden_ps, att_done, o_ps, x2_done = sem("den_inv"), sem("rden_ps"), sem("att_done"), sem("o_ps"), sem("x2_done")
        stats2, rstd2, xn2_done = sem("stats2"), sem("rstd2"), sem("xn2_done")
        xn2t_ps, xn2t_read, xh_done, xl_done = sem("xn2t_ps"), sem("xn2t_read"), sem("xh_done"), sem("xl_done")
        r_ps, r_exp, r_step = sem("r_ps"), sem("r_exp"), sem("r_step")
        g_step, g_last = sem("g_step"), sem("g_last")
        gt_ps, gt_read = sem("gt_ps"), sem("gt_read")
        u_ps, gate_ps, u_gelu, hid_done = sem("u_ps"), sem("gate_ps"), sem("u_gelu"), sem("hid_done")
        hid_hi, hid_lo, d_ps, d_read, y_ps, y_done = (sem("hid_hi"), sem("hid_lo"), sem("d_ps"), sem("d_read"),
                                                      sem("y_ps"), sem("y_done"))
        out_done, unused = sem("out_done"), sem("unused")
        RSTEPS = 11

        block = stack.enter_context(nc.Block())

        def apart(eng):
            eng.sem_inc(unused, 1)

        def attention(eng, turn_of):
            for i in range(LAST_LAG):
                turn_of(Turn(i, i, NB))
            with eng.Fori(0, (NB - LAST_LAG) // 2) as k:
                for u in range(2):
                    turn_of(Turn(k * 2 + (LAST_LAG + u), LAST_LAG + u, NB))
            for i in range(NB, NB + LAST_LAG):
                turn_of(Turn(i, i, NB))

        early = dict(((NB + 2 + i, t), 5 * i + m) for i, units in enumerate(((1, 3, 5, 7, 9), (0, 2, 4, 6, 7, 9)))
                     for m, t in enumerate(units))

        def early_chunk(turn, t):
            m = early.get((turn.at, t)) if isinstance(turn.at, int) else None
            return None if m is None else divmod(m, NCH)

        def projection(turn, t, unit):
            if isinstance(turn.at, int) and turn.at < 2:
                return {(0, unit): Turn(0, 0, NB), (0, UNITS - 1): Turn(1, 1, NB)}.get((turn.at, t))
            return turn if t == unit and turn.batch(0) is not None else None

        xn_units = {(1, 4): 1, (1, 7): 2, (1, 10): 3}

        users = {
            BANK_A: [("qk", 0, qk_less, 2, 2), ("router", 4, r_step, RSTEPS, 5), ("v", 1, v_read, 1, 1), ("gates", 4, gt_read, 1, 2)],
            BANK_B: [("max1", 2, mt_read, 2, 2), ("xn2", 4, xh_done, 1, 1), ("max0", 1, mt_read, 2, 1), ("rden", 3, att_done, 1, 1),
                     ("o", 3, x2_done, 1, 1)],
        }

        def bank_free(turn, bank, step):
            order = users[bank]
            at = [u[0] for u in order].index(step)
            for back in range(1, 3 * len(order)):
                name, lag, reader, per, which = order[(at - back) % len(order)]
                c = Turn(turn.at - (0 if back <= at else 1 + (back - at - 1) // len(order)), 0, NB).batch(lag)
                if c is not None:
                    return reader, count(per * c + which)
            return None

        @block.sync
        def _(sp):
            def load_x(q):
                sp.dma_start(x2[:, 4 * q:4 * q + 4, :], x_v[:, 4 * q:4 * q + 4, :]).then_inc(x_in[q], 16)

            def load_ctx(c, side, done):
                start = c * S
                sp.dma_start(ctx2[side][:, :], ctx_t[:, bass.ds(start, S)]).then_inc(done, 16)

            load_x(0)
            sp.dma_start(id_f[:, :], ident).then_inc(id_in, 16)
            for dst, src in ((wq_sb, wq_t), (wk_sb, wk_t), (bq_sb, bq), (bk_sb, bk)):
                sp.dma_start(dst[:, :], src).then_inc(w_in, 16)

            def operands(c, side, half):
                heads = slice(half * H // 2, (half + 1) * H // 2)
                rows = slice(half * P // 2, (half + 1) * P // 2)
                if isinstance(c, int) and c < 2:
                    sp.wait_ge(zeros_set[side], 2)
                sp.wait_ge(qk_lo, count(c + 1))
                if isinstance(c, int) and c == 1:
                    sp.wait_ge(m_ps, UNITS // 2 * half + 1)
                apart(sp)
                sp.wait_ge(s_ps, count(UNITS * (c - 2) + UNITS // 2 * (half + 1)))
                qk = qk2[side]
                for n, (a, b) in enumerate(PAIRS):
                    sp.dma_start(qk_op[side][DH * n:DH * n + DH, heads, :, :], qk[rows, a:b + 1:b - a, :]).then_inc(op_in[half], 16)

            def maxima(c, side, half):
                heads = slice(half * H // 2, (half + 1) * H // 2)
                sp.wait_ge(mt_read, count(2 * c + 1 + half))
                sp.dma_start(q_op[side][MROW0:MROW0 + MROWS, heads, :], m_t[half][:, :]).then_inc(m_in[half], 16)

            def turn_of(turn):
                c = turn.batch(0)
                if c is not None and not (isinstance(c, int) and c < 2):
                    sp.wait_ge(v_ps, count(c - 1))
                    apart(sp)
                    load_ctx(c, turn.side(0), ctx_in)
                if isinstance(c, int) and c == 0:
                    load_ctx(0, 0, ctx_in)
                    load_ctx(1, 1, ctx1_in)
                    for dst, src in ((id_b, ident_bf), (fut, future), (wv_sb, wv_t), (bv_sb, bv), (wo_sb, wo_t),
                                     (rw_sb, router_t), (hrow, head_rows), (exno, expert_no.partition_broadcast(P)),
                                     (bo_sb, bo.partition_broadcast(P))):
                        sp.dma_start(dst[:, :], src).then_inc(c_in, 16)
                    for q in range(1, 4):
                        load_x(q)
                    for dst, src in ((up_f[:, 0:P], sup_t), (up_f[:, P:NCH * P], rup_t), (dn_f[:, 0:E], sdown),
                                     (dn_f[:, E:NCH * E].rearrange("p (c h) -> p c h", h=E), rdown), (spr[:, :, :], spread)):
                        sp.dma_start(dst, src).then_inc(ff_in, 16)
                c = turn.batch(1)
                if c is not None:
                    operands(c, turn.side(1), 1)
                c = turn.batch(2)
                if c is not None:
                    maxima(c, turn.side(2), 1)
                c = turn.batch(3)
                if c is not None:
                    sp.wait_ge(pv_read, count(2 * c + 2))
                    sp.wait_ge(den_inv, count(c))
                    sp.dma_start(den[:, :], o_raw[1:P:VW, :, :]).then_inc(den_in, 16)
                    sp.wait_ge(att_done, count(c))
                    sp.dma_start(num[:, :], o_raw[0:P:VSTEP, :, :]).then_inc(num_in, 16)
                c = turn.batch(3)
                if c is not None:
                    sp.wait_ge(den_inv, count(c + 1))
                    sp.wait_ge(rden_ps, count(c))
                    sp.dma_start(rden_h[:, :], rden[:, :]).then_inc(rden_in, 16)
                c = turn.batch(0)
                if c is not None:
                    operands(c, turn.side(0), 0)
                c = turn.batch(1)
                if c is not None:
                    maxima(c, turn.side(1), 0)

            attention(sp, turn_of)

            with sp.Fori(0, NCT) as n:
                sp.wait_ge(y_done, n + 2)
                apart(sp)
                sp.dma_start(out_v[:, bass.ds(n * (BANK // P), BANK // P), :], y).then_inc(out_done, 16)
            sp.wait_ge(out_done, 16 * (NCT + 1))

        @block.gpsimd
        def _(pool):
            nc.gpsimd.memset(zero[:, :], 0.0).then_inc(zero_set, 1)
            nc.gpsimd.memset(halfs[:, :], -0.5).then_inc(half_set, 1)
            nc.gpsimd.memset(ones[:, :], 1.0).then_inc(ones_set, 1)
            nc.gpsimd.memset(ones_b[:, :], 1.0).then_inc(ones_set, 1)

            def rstd_1(q):
                tiles = slice(4 * q, 4 * q + 4)
                pool.wait_ge(stats1, 8 * q + 8)
                nc.gpsimd.tensor_scalar(var1[:, tiles], mv1[:, tiles, 1], 1e-5, None, ALU.add).then_inc(rstd1, 1)
                pool.wait_ge(rstd1, 2 * q + 1)
                nc.gpsimd.tensor_tensor(rs1[:, tiles], var1[:, tiles], halfs[:, tiles], ALU.pow).then_inc(rstd1, 1)

            def lo_part(dst, full, high, n=slice(None)):
                return nc.gpsimd.tensor_tensor(dst[:, n], full[:, n], high[:, n].bitcast(F32), ALU.subtract)

            def select(c, t):
                g, u = divmod(t, 3)
                pool.wait_ge(s_exp, count(UNITS * c + t + 1))
                apart(pool)
                if u < 2:
                    v = probs[g][:, u * BANK:(u + 1) * BANK].rearrange("p (j q) -> p j q", j=2)[:, :, 0:P]
                else:
                    v = probs[g][:, J * S:J * S + J * P].rearrange("p (j q) -> p j q", j=J)
                nc.gpsimd.affine_select(out=v, in_=v, compare_op=ALU.is_ge, fill=0.0, base=0,
                                        pattern=[[0, v.shape[1]], [1, P]], channel_multiplier=-1).then_inc(s_mask, 1)

            def add_bo(q):
                tiles = slice(4 * q, 4 * q + 4)
                pool.wait_ge(xn_done, 4 * q + 4)
                pool.wait_ge(c_in, 16 * 9)
                nc.gpsimd.tensor_tensor(x2[:, tiles, :], x2[:, tiles, :],
                                        bo_sb[:, :].unsqueeze(1).to_broadcast([P, 4, E]), ALU.add).then_inc(resid, 1)

            def project(turn):
                c = turn.batch(0)
                qk = qk2[turn.side(0)]
                pool.wait_ge(qk_mid, count(c + 1))
                nc.gpsimd.tensor_tensor(qk[:, 2:6:3, :], qk_res[:, :, :], qk[:, 1:5:3, :], ALU.subtract).then_inc(qk_lo, 1)

            def turn_of(turn):
                for t in range(UNITS):
                    c = turn.batch(4)
                    if t == 0 and c is not None:
                        pool.wait_ge(stats2, count(4 * c + 4))
                        apart(pool)
                        nc.gpsimd.tensor_scalar(var2[:, :], mv2[:, :, 1], 1e-5, None, ALU.add).then_inc(rstd2, 1)
                        pool.wait_ge(rstd2, count(2 * c + 1))
                        nc.gpsimd.tensor_tensor(rs2[:, :], var2[:, :], halfs[:, 0:QB], ALU.pow).then_inc(rstd2, 1)
                    if t == 10 and c is not None:
                        pool.wait_ge(r_step, count(RSTEPS * (c + 1)))
                        apart(pool)
                        nc.gpsimd.tensor_copy(g_parts[:, :, 0, :], gate[:, :, :]).then_inc(g_step, 1)
                        pool.wait_ge(g_step, count(3 * c + 1))
                        nc.gpsimd.tensor_tensor(gres[:, :, :], gate[:, :, :], g_parts[:, :, 0, :], ALU.subtract).then_inc(g_step, 1)
                        pool.wait_ge(g_step, count(3 * c + 2))
                        apart(pool)
                        nc.gpsimd.tensor_copy(g_parts[:, :, 1, :], gres[:, :, :]).then_inc(g_step, 1)
                        pool.wait_ge(g_step, count(3 * c + 3))
                        nc.gpsimd.tensor_tensor(g_parts[:, :, 2, :], gres[:, :, :], g_parts[:, :, 1, :], ALU.subtract)\
                            .then_inc(g_last, 1)
                    c = turn.batch(2)
                    if c is not None:
                        select(c, t)
                    if isinstance(turn.at, int) and turn.at == 2 and t % 3 == 2:
                        add_bo(t // 3)
                    if isinstance(turn.at, int) and (turn.at, t) == (0, 9):
                        for q in range(1, 4):
                            rstd_1(q)
                    p = projection(turn, t, QK_TICK + 1)
                    if p is not None:
                        project(p)
                    c = turn.batch(4)
                    if t == 6 and c is not None:
                        pool.wait_ge(xh_done, count(c + 1))
                        nc.gpsimd.tensor_tensor(xl[:, bass.ds(c * S, S)], xn2_t[:, :],
                                                xh[:, bass.ds(c * S, S)].bitcast(F32), ALU.subtract).then_inc(xl_done, 1)
                if not isinstance(turn.at, int):
                    return
                if turn.at == 0:
                    pool.wait_ge(ones_set, 2)
                    for side in range(2):
                        pool.wait_ge(zeros_set[side], 2)
                        pool.dma_start(k_op[side][MROW0:MROW0 + MROWS, :, :], ones_b[:, :]).then_inc(ones_in, 16)
                    pool.wait_ge(w_hi, 1)
                    lo_part(up_l, up_f, up_h).then_inc(w_lo, 1)
                if turn.at == 1:
                    pool.wait_ge(w_hi, 2)
                    lo_part(dn_l, dn_f, dn_h).then_inc(w_lo, 1)

            pool.wait_ge(half_set, 1)
            nc.gpsimd.memset(qk_op[0][:, 0:H // 2, :, :].bitcast(F32), 0.0).then_inc(zeros_set[0], 1)
            rstd_1(0)
            nc.gpsimd.memset(qk_op[0][:, H // 2:H, :, :].bitcast(F32), 0.0).then_inc(zeros_set[0], 1)
            attention(pool, turn_of)

        @block.scalar
        def _(act):
            act.sem_inc(gt_read, 1)

            def zeros_1(half):
                nc.scalar.copy(qk_op[1][:, half * H // 2:(half + 1) * H // 2, :, :].rearrange("p h n s -> p (h n s)"),
                               zero[:, :].to_broadcast([P, H * S])).then_inc(zeros_set[1], 1)

            act.wait_ge(zero_set, 1)
            nc.scalar.activation(first_exp[:, :], zero[:, :], ACT.Exp).then_inc(unused, 1)
            zeros_1(0)

            def gelu(n, k):
                at = n * NCH + k
                act.wait_ge(u_ps, at + 1)
                act.wait_ge(hid_done, count(at - NF + 1) if isinstance(at, int) else at - NF + 1)
                nc.scalar.activation(gel[k % NF], psum[:, k % NF, :], ACT.Gelu).then_inc(u_gelu, 1)

            def high(n, k):
                at = n * NCH + k
                act.wait_ge(hid_done, at + 1)
                act.wait_ge(d_ps, count(at - NF + 1) if isinstance(at, int) else at - NF + 1)
                nc.scalar.copy(hid_h[k % NF][:, :], hid[k % NF]).then_inc(hid_hi, 1)

            def read_d(n):
                act.wait_ge(d_ps, (n + 1) * NCH)
                act.wait_ge(y_ps, n + 1)
                nc.scalar.copy(y_t, psum[:, 5, :]).then_inc(d_read, 1)

            def chunk(n, k, first):
                gelu(n, k)
                if k > 0:
                    high(n, k - 1)
                elif not first:
                    high(n - 1, NCH - 1)
                if k == 1 and not first:
                    read_d(n - 1)

            def read_xn(q):
                act.wait_ge(xnt_ps, q + 1)
                nc.scalar.copy(xn_t[:, BANK * q:BANK * (q + 1)], psum[:, BANK_PV - q % 2, :]).then_inc(xnt_read, 1)

            def read_pv(c, n):
                act.wait_ge(pv_ps, count(G * c + 2 * n + 2))
                act.wait_ge(num_in, count(16 * c))
                act.wait_ge(den_in, count(16 * c))
                nc.scalar.copy(o_raw[:, 2 * n:2 * n + 2, :].rearrange("p g q -> p (g q)"), psum[:, BANK_PV, :])\
                    .then_inc(pv_read, 1)

            def read_maxima(c, half):
                act.wait_ge(mt_ps, count(2 * c + 1 + half))
                act.wait_ge(m_in[half], count(16 * c))
                nc.scalar.copy(m_t[half][:, :], psum[0:MROWS * H // 2, BANK_B, 0:S // 2].bitcast(BF16)).then_inc(mt_read, 1)

            def project(turn):
                c = turn.batch(0)
                act.wait_ge(qk_ps, count(c + 1))
                for half in range(2):
                    act.wait_ge(op_in[half], count(96 * (c - 1)))
                if isinstance(c, int) and c == 0:
                    act.wait_ge(w_in, 64)
                for n, bias in enumerate((bq_sb, bk_sb)):
                    nc.scalar.activation(qk2[turn.side(0)][:, 3 * n, :], psum[:, BANK_A, S * n:S * n + S], ACT.Identity,
                                         bias=bias[:, :]).then_inc(qk_hi, 1)

            def turn_of(turn):
                for t in range(UNITS):
                    c = turn.batch(2)
                    if c is not None:
                        g, u = divmod(t, 3)
                        act.wait_ge(s_ps, count(UNITS * c + t + 1))
                        nc.scalar.activation(probs[g][:, u * BANK:(u + 1) * BANK], psum[:, BANK_S + t % SB, :], ACT.Exp,
                                             scale=float(DH) ** -0.5).then_inc(s_exp, 1)
                    if t == 0 and c is not None:
                        read_maxima(c, 1)
                    c = turn.batch(3)
                    if t == 1 and c is not None:
                        read_pv(c, 1)
                    if isinstance(turn.at, int) and (turn.at, t) == (0, 9):
                        zeros_1(1)
                    p = projection(turn, t, QK_TICK)
                    if p is not None:
                        project(p)
                    c = turn.batch(4)
                    if t == 3 and c is not None:
                        act.wait_ge(xn2t_ps, count(c + 1))
                        nc.scalar.copy(xn2_t[:, :], psum[:, BANK_B, 0:S]).then_inc(xn2t_read, 1)
                        nc.scalar.copy(xh[:, bass.ds(c * S, S)], psum[:, BANK_B, 0:S]).then_inc(xh_done, 1)
                    c = turn.batch(1)
                    if t == 7 and c is not None:
                        read_maxima(c, 0)
                    c = turn.batch(2)
                    if t == 9 and c is not None:
                        read_pv(c, 0)
                    c = turn.batch(4)
                    if t == 7 and c is not None:
                        act.wait_ge(r_step, count(RSTEPS * c + 5))
                        nc.scalar.activation(ex[:, :, :], lgm[:, :, :], ACT.Exp).then_inc(r_exp, 1)
                    c = turn.batch(1)
                    if t == 10 and c is not None:
                        act.wait_ge(v_ps, count(c + 1))
                        act.wait_ge(pv_ps, count(G * (c - 1)))
                        if isinstance(c, int) and c < 2:
                            act.wait_ge(v_ones_set, 2)
                        nc.scalar.copy(v_op[turn.side(1)][:, :, :, 0:VW:VSTEP],
                                       psum[:, BANK_A, 0:QB * P].rearrange("p (a h d) -> p a h d", a=QB, h=H)).then_inc(v_read, 1)
                    c = turn.batch(4)
                    if t == 11 and c is not None:
                        act.wait_ge(gt_ps, count(c + 1))
                        nc.scalar.copy(gate_t[:, bass.ds(c * S, S)], psum[0:3 * NR, BANK_A, 0:S // 2].bitcast(BF16))\
                            .then_inc(gt_read, 1)
                    if isinstance(turn.at, int) and (turn.at, t) in xn_units:
                        read_xn(xn_units[turn.at, t])
                    at = early_chunk(turn, t)
                    if at == (1, 0):
                        act.wait_ge(num_in, 16 * NB)
                        act.wait_ge(den_in, 16 * NB)
                    if at is not None:
                        chunk(*at, at[0] == 0)
                if not isinstance(turn.at, int):
                    return
                if turn.at == 0:
                    act.wait_ge(ff_in, 16 * 5)
                    nc.scalar.copy(up_h[:, :], up_f).then_inc(w_hi, 1)
                    nc.scalar.copy(dn_h[:, :], dn_f).then_inc(w_hi, 1)
                if turn.at == 1:
                    act.wait_ge(w_lo, 2)

            read_xn(0)
            attention(act, turn_of)

            for k in range(len(early) - NCH, NCH):
                chunk(1, k, False)
            with act.Fori(2, NCT) as n:
                for k in range(NCH):
                    chunk(n, k, False)
            high(NCT - 1, NCH - 1)
            read_d(NCT - 1)

        @block.vector
        def _(dve):
            def gated(n, k):
                at = n * NCH + k
                dve.wait_ge(u_gelu, at + 1)
                dve.wait_ge(hid_lo, count(at - NF + 1) if isinstance(at, int) else at - NF + 1)
                if k == 0:
                    nc.vector.tensor_copy(hid[k % NF], gel[k % NF]).then_inc(hid_done, 1)
                else:
                    dve.wait_ge(gate_ps, (NCH - 1) * n + k)
                    nc.vector.tensor_tensor(hid[k % NF], gel[k % NF], psum[:, 3 + k % 2, :], ALU.mult)\
                        .then_inc(hid_done, 1)

            def low(n, k):
                at = n * NCH + k
                dve.wait_ge(hid_hi, at + 1)
                dve.wait_ge(d_ps, count(at - NF + 1) if isinstance(at, int) else at - NF + 1)
                nc.vector.tensor_tensor(hid_l[k % NF][:, :], hid[k % NF], hid_h[k % NF][:, :].bitcast(F32),
                                        ALU.subtract).then_inc(hid_lo, 1)

            def finish(n):
                dve.wait_ge(y_ps, n + 2)
                dve.wait_ge(out_done, 16 * (n + 1))
                nc.vector.tensor_tensor(y, psum[:, BANK_B, :].rearrange("p (a e) -> p a e", e=E),
                                        x2[:, bass.ds(n * (BANK // P), BANK // P), :], ALU.add).then_inc(y_done, 1)

            def chunk(n, k, first):
                gated(n, k)
                if k > 0:
                    low(n, k - 1)
                elif not first:
                    low(n - 1, NCH - 1)
                if k == 3 and not first:
                    finish(n - 1)

            def stats_1(q):
                dve.wait_ge(x_in[q], 16)
                for a in range(4 * q, 4 * q + 4):
                    nc.vector.bn_stats(st1[:, a, :], x2[:, a, :]).then_inc(stats1, 1)
                for a in range(4 * q, 4 * q + 4):
                    dve.wait_ge(stats1, 8 * q + a % 4 + 1)
                    nc.vector.bn_aggr(mv1[:, a, :], st1[:, a, :]).then_inc(stats1, 1)
                dve.wait_ge(stats1, 8 * q + 8)

            def apply_1(q):
                dve.wait_ge(rstd1, 2 * q + 2)
                for a in range(4 * q, 4 * q + 4):
                    nc.vector.tensor_scalar(xn[:, a, :], x2[:, a, :], mv1[:, a, 0:1], rs1[:, a:a + 1],
                                            ALU.subtract, ALU.mult).then_inc(xn_done, 1)

            def split_maxima(c, side, half):
                heads = slice(half * H // 2, (half + 1) * H // 2)
                m = mx[side][:, :, heads]
                high, low = (m_parts[half][:, :, n, :] for n in range(2))
                dve.wait_ge(m_max, count(UNITS * c + UNITS // 2 * (half + 1)))
                dve.wait_ge(mt_ps, count(2 * c - 1 + half))
                nc.vector.tensor_scalar(high, m, -1.0, None, ALU.mult).then_inc(m_split, 1)
                dve.wait_ge(m_split, count(4 * c + 2 * half + 1))
                nc.vector.scalar_tensor_tensor(low, m, -1.0, high, ALU.mult, ALU.subtract).then_inc(m_split, 1)

            def choose(c, t):
                def after(n):
                    dve.wait_ge(r_step, count(RSTEPS * c + n))

                lg = psum[:, BANK_A, 0:QB * NR].rearrange("p (a r) -> p a r", a=QB)
                if t == 6:
                    dve.wait_ge(r_ps, count(c + 1))
                    apart(dve)
                    for a in range(QB):
                        nc.vector.max(top[:, a, :], lg[:, a, :]).then_inc(r_step, 1)
                    after(2)
                    apart(dve)
                    for a in range(QB):
                        nc.vector.max_index(top_i[:, a, :], top[:, a, :], lg[:, a, :]).then_inc(r_step, 1)
                    nc.vector.tensor_tensor(lgm[:, :, :], lg, top[:, :, 0:1].to_broadcast([P, QB, NR]), ALU.subtract)\
                        .then_inc(r_step, 1)
                if t == 7:
                    after(4)
                    nc.vector.tensor_tensor(
                        is_top[:, :, :, :], exno[:, :].unsqueeze(1).unsqueeze(3).to_broadcast([P, QB, NR, TOPK]),
                        top_i[:, :, 0:TOPK].unsqueeze(2).to_broadcast([P, QB, NR, TOPK]), ALU.is_equal).then_inc(r_step, 1)
                if t == 8:
                    after(6)
                    nc.vector.tensor_reduce(chosen[:, :, :], is_top[:, :, :, :], AX, ALU.add).then_inc(r_step, 1)
                    dve.wait_ge(r_exp, count(c + 1))
                    nc.vector.tensor_reduce(exs[:, :], ex[:, :, :], AX, ALU.add).then_inc(r_step, 1)
                if t == 9:
                    after(8)
                    nc.vector.reciprocal(rexs[:, :], exs[:, :]).then_inc(r_step, 1)
                    nc.vector.tensor_tensor(gsel[:, :, :], ex[:, :, :], chosen[:, :, :], ALU.mult).then_inc(r_step, 1)
                    after(10)
                    nc.vector.tensor_tensor(gate[:, :, :], gsel[:, :, :], rexs[:, :].unsqueeze(2).to_broadcast([P, QB, NR]),
                                            ALU.mult).then_inc(r_step, 1)

            def project(turn):
                c = turn.batch(0)
                qk = qk2[turn.side(0)]
                dve.wait_ge(qk_lo, count(c))
                dve.wait_ge(qk_hi, count(2 * c + 2))
                for n, bias in enumerate((bq_sb, bk_sb)):
                    nc.vector.scalar_tensor_tensor(qk_res[:, n, :], psum[:, BANK_A, S * n:S * n + S], bias[:, :],
                                                   qk[:, 3 * n, :], ALU.add, ALU.subtract).then_inc(qk_less, 1)
                dve.wait_ge(qk_less, count(2 * c + 2))
                nc.vector.tensor_copy(qk[:, 1:5:3, :], qk_res[:, :, :]).then_inc(qk_mid, 1)

            def turn_of(turn):
                for t in range(UNITS):
                    c = turn.batch(1)
                    if c is not None:
                        g, u = divmod(t, 3)
                        dve.wait_ge(m_ps, count(UNITS * c + t + 1))
                        if u < 2:
                            src = psum[:, BANK_M + t % MB, :].rearrange("p (j k) -> p j k", j=2)
                            dst = mx[turn.side(1)][:, 1, J * g + 2 * u:J * g + 2 * u + 2]
                        else:
                            src = psum[:, BANK_M + t % MB, :].rearrange("p (j k) -> p j k", j=J)
                            dst = mx[turn.side(1)][:, 0, J * g:J * g + J]
                        nc.vector.tensor_reduce(dst, src, AX, ALU.max).then_inc(m_max, 1)
                        if t in (5, 11):
                            split_maxima(c, turn.side(1), t // 6)
                    c = turn.batch(4)
                    if t == 1 and c is not None:
                        dve.wait_ge(rstd2, count(2 * c + 2))
                        for a in range(QB):
                            nc.vector.tensor_scalar(xn2[:, a, :], x2[:, bass.ds(c * QB + a, 1), :].rearrange("p a e -> p (a e)"),
                                                    mv2[:, a, 0:1], rs2[:, a:a + 1], ALU.subtract, ALU.mult)\
                                .then_inc(xn2_done, 1)
                    if isinstance(turn.at, int) and (turn.at, t) == (0, 9):
                        for q in range(1, 4):
                            stats_1(q)
                    p = projection(turn, t, QK_TICK + 1)
                    if p is not None:
                        project(p)
                    c = turn.batch(4)
                    if t >= 6 and c is not None:
                        choose(c, t)
                    c = turn.batch(3)
                    if t == 4 and c is not None:
                        dve.wait_ge(den_in, count(16 * (c + 1)))
                        dve.wait_ge(rden_in, count(16 * c))
                        nc.vector.reciprocal(rden[:, :], den[:, :]).then_inc(den_inv, 1)
                    if t == 10 and c is not None:
                        dve.wait_ge(rden_ps, count(c + 1))
                        dve.wait_ge(num_in, count(16 * (c + 1)))
                        dve.wait_ge(o_ps, count(c))
                        nc.vector.tensor_tensor(att[:, :], psum[:, BANK_B, 0:S], num[:, :], ALU.mult).then_inc(att_done, 1)
                    c = turn.batch(3)
                    if t == 11 and c is not None:
                        dve.wait_ge(o_ps, count(c + 1))
                        dve.wait_ge(resid, 4)
                        rows = x2[:, bass.ds(c * QB, QB), :]
                        nc.vector.tensor_tensor(rows, psum[:, BANK_B, 0:QB * P].rearrange("p (a e) -> p a e", a=QB), rows,
                                                ALU.add).then_inc(x2_done, 1)
                        dve.wait_ge(x2_done, count(c + 1))
                        dve.wait_ge(rstd2, count(2 * c))
                        apart(dve)
                        for a in range(QB):
                            nc.vector.bn_stats(st2[:, a, :], x2[:, bass.ds(c * QB + a, 1), :].rearrange("p a e -> p (a e)"))\
                                .then_inc(stats2, 1)
                        for a in range(QB):
                            dve.wait_ge(stats2, count(4 * c + a + 1))
                            apart(dve)
                            nc.vector.bn_aggr(mv2[:, a, :], st2[:, a, :]).then_inc(stats2, 1)
                    if isinstance(turn.at, int) and turn.at == 1 and t in (3, 6):
                        apply_1(1 + t // 3)
                    at = early_chunk(turn, t)
                    if at is not None:
                        chunk(*at, at[0] == 0)
                if isinstance(turn.at, int) and turn.at == 0:
                    apply_1(1)

            for side in range(2):
                nc.vector.memset(v_op[side][:, :, :, :], 1.0).then_inc(v_ones_set, 1)
            stats_1(0)
            apply_1(0)
            attention(dve, turn_of)

            for k in range(len(early) - NCH, NCH):
                chunk(1, k, False)
            with dve.Fori(2, NCT) as n:
                for k in range(NCH):
                    chunk(n, k, False)
            low(NCT - 1, NCH - 1)
            finish(NCT - 1)

        @block.tensor
        def _(pe):
            mm = nc.tensor.matmul

            def wait_bank(turn, bank, step):
                got = bank_free(turn, bank, step)
                if got is not None:
                    pe.wait_ge(*got)

            def up(n, k):
                at = n * NCH + k
                cols = bass.ds(n * BANK, BANK)
                w = slice(P * k, P * k + P)
                pe.wait_ge(u_gelu, count(at - NF + 1) if isinstance(at, int) else at - NF + 1)
                mm(psum[:, k % NF, :], up_h[:, w], xh[:, cols], start=True, stop=False)
                mm(psum[:, k % NF, :], up_h[:, w], xl[:, cols], start=False, stop=False)
                mm(psum[:, k % NF, :], up_l[:, w], xh[:, cols], start=False, stop=True).then_inc(u_ps, 1)
                if k > 0:
                    pe.wait_ge(hid_done, count(at - 1) if isinstance(at, int) else at - 1)
                    apart(pe)
                    mm(psum[:, 3 + k % 2, :], spr[:, k - 1, :], gate_t[:, cols], start=True, stop=True).then_inc(gate_ps, 1)

            def down(n, k):
                at = n * NCH + k
                w = slice(E * k, E * k + E)
                if k == 0:
                    pe.wait_ge(d_read, n)
                pe.wait_ge(hid_hi, at + 1)
                mm(psum[:, 5, :], dn_h[:, w], hid_h[k % NF][:, :], start=(k == 0), stop=False)
                mm(psum[:, 5, :], dn_l[:, w], hid_h[k % NF][:, :], start=False, stop=False)
                pe.wait_ge(hid_lo, at + 1)
                mm(psum[:, 5, :], dn_h[:, w], hid_l[k % NF][:, :], start=False, stop=(k == NCH - 1)).then_inc(d_ps, 1)

            def transpose_y(n):
                pe.wait_ge(d_read, n + 1)
                pe.wait_ge(y_done, n + 1)
                for a in range(BANK // P):
                    last = nc.tensor.transpose(psum[:, BANK_B, P * a:P * a + P], y_t[:, P * a:P * a + P], id_f[:, :])
                last.then_inc(y_ps, 1)

            def chunk(n, k, first):
                up(n, k)
                if k >= 2:
                    down(n, k - 2)
                elif not first:
                    down(n - 1, NCH - 2 + k)
                if k == 2 and not first:
                    transpose_y(n - 1)

            def transpose_xn(q):
                pe.wait_ge(xn_done, 4 * q + 4)
                if q >= 2:
                    pe.wait_ge(xnt_read, q - 1)
                for a in range(4):
                    last = nc.tensor.transpose(psum[:, BANK_PV - q % 2, P * a:P * a + P], xn[:, 4 * q + a, :], id_f[:, :])
                last.then_inc(xnt_ps, 1)

            def max_unit(c, side, t):
                g, u = divmod(t, 3)
                if t % 6 == 0:
                    pe.wait_ge(op_in[t // 6], count(96 * (c + 1)))
                pe.wait_ge(m_max, count(UNITS * c + t - MB + 1))
                bank = psum[:, BANK_M + t % MB, :]
                if u < 2:
                    heads = [J * g + 2 * u, J * g + 2 * u + 1]
                    v = bank.rearrange("p (j k) -> p j k", j=2)
                    mm(v[:, :, P:2 * P], id_b[:, :], fut[:, :].unsqueeze(1).to_broadcast([P, 2, P]), start=True, stop=False,
                       skip_group_check=True)
                    for n, h in enumerate(heads):
                        last = mm(v[:, n, :], q_op[side][0:MROW0, h, P:2 * P], k_op[side][0:MROW0, h, :], start=False,
                                  stop=(n == 1), skip_group_check=True)
                else:
                    v = bank.rearrange("p (j k) -> p j k", j=J)
                    mm(v, id_b[:, :], fut[:, :].unsqueeze(1).to_broadcast([P, J, P]), start=True, stop=False,
                       skip_group_check=True)
                    for n in range(J):
                        last = mm(v[:, n, :], q_op[side][0:MROW0, J * g + n, 0:P], k_op[side][0:MROW0, J * g + n, 0:P],
                                  start=False, stop=(n == J - 1), skip_group_check=True)
                last.then_inc(m_ps, 1)

            def exp_unit(c, side, t):
                g, u = divmod(t, 3)
                if t % 6 == 0:
                    pe.wait_ge(m_in[t // 6], count(16 * (c + 1)))
                pe.wait_ge(s_exp, count(UNITS * c + t - SB + 1))
                bank = psum[:, BANK_S + t % SB, :]
                if u < 2:
                    for n in range(2):
                        h = J * g + 2 * u + n
                        last = mm(bank[:, S * n:S * n + S], k_op[side][:, h, 0:P], q_op[side][:, h, :], start=True, stop=True)
                else:
                    for n in range(J):
                        h = J * g + n
                        last = mm(bank[:, P * n:P * n + P], k_op[side][:, h, P:2 * P], q_op[side][:, h, P:2 * P],
                                  start=True, stop=True)
                last.then_inc(s_ps, 1)

            def pv(c, side, g):
                pe.wait_ge(s_mask, count(UNITS * c + 3 * g + 3))
                if g == 0:
                    pe.wait_ge(v_read, count(c + 1))
                if g % 2 == 0:
                    pe.wait_ge(pv_read, count(2 * c + g // 2))
                col = S * (g % 2)
                bank = psum[:, BANK_PV, :]
                for j in range(J):
                    mm(bank[32 * j:32 * j + 32, col:col + S], v_op[side][:, 0, J * g + j, :],
                       probs[g][:, S * j:S * j + S], start=True, stop=False)
                for j in range(J):
                    last = mm(bank[32 * j:32 * j + 32, col + P:col + S], v_op[side][:, 1, J * g + j, :],
                              probs[g][:, J * S + P * j:J * S + P * j + P], start=False, stop=True)
                last.then_inc(pv_ps, 1)

            def transpose_maxima(turn, c, half):
                pe.wait_ge(m_split, count(4 * c + 2 * half + 2))
                wait_bank(turn, BANK_B, f"max{half}")
                apart(pe)
                bank = psum[:, BANK_B, :].bitcast(BF16)
                for a in range(QB):
                    last = nc.tensor.transpose(bank[0:MROWS * H // 2, P * a:P * a + P],
                                               m_parts[half][:, a, :, :].rearrange("p m h -> p (m h)"), id_b[:, :])
                last.then_inc(mt_ps, 1)

            def project(turn):
                c = turn.batch(0)
                if isinstance(c, int) and c < 2:
                    pe.wait_ge((ctx_in, ctx1_in)[c], 16)
                else:
                    pe.wait_ge(ctx_in, 16 * c)
                if isinstance(c, int) and c % 2 == 0:
                    pe.wait_ge(xnt_read, c // 2 + 1)
                wait_bank(turn, BANK_A, "qk")
                mm(psum[:, BANK_A, 0:S], wq_sb[:, :], xn_t[:, bass.ds(c * S, S)], start=True, stop=True)
                mm(psum[:, BANK_A, S:2 * S], wk_sb[:, :], ctx2[turn.side(0)][:, :], start=True, stop=True)\
                    .then_inc(qk_ps, 1)

            def turn_of(turn):
                for t in range(UNITS):
                    c = turn.batch(1)
                    if c is not None:
                        max_unit(c, turn.side(1), t)
                    c = turn.batch(2)
                    if c is not None:
                        exp_unit(c, turn.side(2), t)
                        if t in (5, 8, 11):
                            pv(c, turn.side(2), (t - 5) // 3)
                        if t == 0:
                            transpose_maxima(turn, c, 1)
                    c = turn.batch(3)
                    if t == 1 and c is not None:
                        pv(c, turn.side(3), 3)
                    p = projection(turn, t, QK_TICK)
                    if p is not None:
                        project(p)
                    c = turn.batch(4)
                    if t == 3 and c is not None:
                        pe.wait_ge(xn2_done, count(QB * (c + 1)))
                        wait_bank(turn, BANK_B, "xn2")
                        for a in range(QB):
                            last = nc.tensor.transpose(psum[:, BANK_B, P * a:P * a + P], xn2[:, a, :], id_f[:, :])
                        last.then_inc(xn2t_ps, 1)
                    if t == 5 and c is not None:
                        pe.wait_ge(xn2t_read, count(c + 1))
                        wait_bank(turn, BANK_A, "router")
                        for a in range(QB):
                            last = mm(psum[:, BANK_A, NR * a:NR * a + NR], xn2_t[:, P * a:P * a + P], rw_sb[:, :],
                                      start=True, stop=True)
                        last.then_inc(r_ps, 1)
                    c = turn.batch(1)
                    if t == 7 and c is not None:
                        transpose_maxima(turn, c, 0)
                    if t == 9 and c is not None:
                        wait_bank(turn, BANK_A, "v")
                        mm(psum[:, BANK_A, 0:QB * P].rearrange("p (a e) -> p a e", a=QB), ones[0:1, 0:P],
                           bv_sb[:, :].unsqueeze(1).to_broadcast([1, QB, P]), start=True, stop=False, skip_group_check=True)
                        for a in range(QB):
                            last = mm(psum[:, BANK_A, P * a:P * a + P], ctx2[turn.side(1)][:, P * a:P * a + P], wv_sb[:, :],
                                      start=False, stop=(a == QB - 1), skip_group_check=True)
                        last.then_inc(v_ps, 1)
                    c = turn.batch(3)
                    if t == 9 and c is not None:
                        pe.wait_ge(rden_in, count(16 * (c + 1)))
                        wait_bank(turn, BANK_B, "rden")
                        mm(psum[:, BANK_B, 0:S], hrow[:, :], rden_h[:, :], start=True, stop=True).then_inc(rden_ps, 1)
                    if t == 11 and c is not None:
                        pe.wait_ge(att_done, count(c + 1))
                        wait_bank(turn, BANK_B, "o")
                        for a in range(QB):
                            last = mm(psum[:, BANK_B, P * a:P * a + P], att[:, P * a:P * a + P], wo_sb[:, :],
                                      start=True, stop=True)
                        last.then_inc(o_ps, 1)
                    c = turn.batch(4)
                    if t == 11 and c is not None:
                        pe.wait_ge(g_last, count(c + 1))
                        wait_bank(turn, BANK_A, "gates")
                        apart(pe)
                        bank = psum[:, BANK_A, :].bitcast(BF16)
                        for a in range(QB):
                            last = nc.tensor.transpose(bank[0:3 * NR, P * a:P * a + P],
                                                       g_parts[:, a, :, :].rearrange("p n r -> p (n r)"), id_b[:, :])
                        last.then_inc(gt_ps, 1)
                    if isinstance(turn.at, int) and (turn.at, t) in xn_units:
                        transpose_xn(xn_units[turn.at, t])
                    at = early_chunk(turn, t)
                    if at == (0, 0):
                        pe.wait_ge(w_lo, 2)
                        pe.wait_ge(ff_in, 16 * 5)
                        pe.wait_ge(xl_done, BANK // S)
                        pe.wait_ge(gt_read, BANK // S + 1)
                        pe.wait_ge(m_max, UNITS * NB)
                        pe.wait_ge(s_exp, UNITS * NB)
                    if at == (0, 1):
                        pe.wait_ge(pv_read, 2 * NB)
                    if at == (1, 0):
                        pe.wait_ge(xl_done, 2 * BANK // S)
                        pe.wait_ge(gt_read, 2 * BANK // S + 1)
                    if at is not None:
                        chunk(*at, at[0] == 0)
                if not isinstance(turn.at, int):
                    return
                if turn.at == 0:
                    pe.wait_ge(c_in, 16 * 9)
                if turn.at == 1:
                    pe.wait_ge(ones_in, 32)
                    pe.wait_ge(xnt_read, 4)

            pe.sem_inc(y_ps, 1)
            pe.sem_inc(y_done, 1)
            pe.sem_inc(out_done, 16)
            pe.wait_ge(id_in, 16)
            transpose_xn(0)
            pe.wait_ge(w_in, 64)
            attention(pe, turn_of)

            pe.wait_ge(xh_done, NB)
            for k in range(len(early) - NCH, NCH):
                chunk(1, k, False)
            pe.wait_ge(xl_done, NB)
            pe.wait_ge(gt_read, NB + 1)
            with pe.Fori(2, NCT) as n:
                for k in range(NCH):
                    chunk(n, k, False)
            down(NCT - 1, NCH - 2)
            down(NCT - 1, NCH - 1)
            transpose_y(NCT - 1)


def kernel(x, ctx_1024, L0_xattn_Wq, L0_xattn_Wk, L0_xattn_Wv, L0_xattn_Wo, L0_xattn_bq, L0_xattn_bk, L0_xattn_bv,
           L0_xattn_bo, L0_ffn_shared_up, L0_ffn_shared_down, L0_ffn_routed_up, L0_ffn_routed_down, L0_ffn_router_w):
    import concourse.bacc as bacc
    import ml_dtypes
    from concourse.bass_utils import run_bass_kernel_spmd

    nb, s, e = x.shape
    heads, dh = 16, 8
    n = np.arange(e).reshape(2, heads // 2, dh).transpose(0, 2, 1).reshape(-1)
    r = np.arange(e).reshape(4, 4, dh).transpose(1, 2, 0).reshape(-1)
    n_routed, ed, _ = L0_ffn_routed_up.shape
    n_shared = L0_ffn_shared_up.shape[0]
    pairs = n_routed // 2
    spread = np.zeros((3, n_routed, pairs, 128), np.float32)
    for c in range(pairs):
        for half in range(2):
            spread[:, 2 * c + half, c, ed * half:ed * half + ed] = 1.0
    head_rows = np.zeros((heads, 4, dh, 4), np.float32)
    for h in range(heads):
        head_rows[h, h // 4, :, h % 4] = 1.0
    future = np.where(np.arange(128)[None, :] > np.arange(128)[:, None], -1e30, 0.0)
    arrays = {
        "x": x,
        "ctx_t": np.asarray(ctx_1024).reshape(nb * s, e).T,
        "wq_t": np.asarray(L0_xattn_Wq)[n].T,
        "wk_t": np.asarray(L0_xattn_Wk)[n].T,
        "wv_t": np.asarray(L0_xattn_Wv).T,
        "wo_t": np.asarray(L0_xattn_Wo)[:, r].T,
        "bq": np.asarray(L0_xattn_bq)[n][:, None],
        "bk": np.asarray(L0_xattn_bk)[n][:, None],
        "bv": np.asarray(L0_xattn_bv)[None, :],
        "bo": L0_xattn_bo,
        "sup_t": np.asarray(L0_ffn_shared_up).reshape(n_shared * ed, e).T,
        "rup_t": np.asarray(L0_ffn_routed_up).reshape(n_routed * ed, e).T,
        "sdown": np.asarray(L0_ffn_shared_down).transpose(0, 2, 1).reshape(n_shared * ed, e),
        "rdown": np.asarray(L0_ffn_routed_down).transpose(0, 2, 1).reshape(pairs, 128, e).transpose(1, 0, 2),
        "router_t": np.asarray(L0_ffn_router_w).T,
        "ident": np.eye(128, dtype=np.float32),
        "ident_bf": np.eye(128).astype(ml_dtypes.bfloat16),
        "future": future.astype(ml_dtypes.bfloat16),
        "spread": spread.reshape(3 * n_routed, pairs, 128).astype(ml_dtypes.bfloat16),
        "expert_no": np.arange(n_routed, dtype=np.float32),
        "head_rows": head_rows.reshape(heads, e),
    }
    nc = bacc.Bacc("TRN2", target_bir_lowering=False, num_devices=1)
    given, args = {}, []
    for name, a in arrays.items():
        a = np.ascontiguousarray(a)
        given[f"in_{name}"] = a
        args.append(nc.dram_tensor(f"in_{name}", a.shape, mybir.dt.from_np(a.dtype), kind="ExternalInput").ap())
    args.append(nc.dram_tensor("out_0", (nb, s, e), mybir.dt.float32, kind="ExternalOutput").ap())
    xattn_moe_kernel(nc, *args)
    got = run_bass_kernel_spmd(nc, [given], core_ids=[0])
    return got.results[0]["out_0"]
```

```python
from contextlib import ExitStack

import numpy as np

import concourse.bass as bass
from concourse import mybir

F32 = mybir.dt.float32
F32R = mybir.dt.float32r
BF16 = mybir.dt.bfloat16
U32 = mybir.dt.uint32
ALU = mybir.AluOpType
ACT = mybir.ActivationFunctionType
AX = mybir.AxisListType.X

P = 128
BANK = 512


class Turn:

    def __init__(self, at, first, batches):
        self.at, self.first, self.batches = at, first, batches

    def batch(self, lag):
        c = self.at - lag
        return None if isinstance(c, int) and not 0 <= c < self.batches else c

    def side(self, lag):
        return (self.first - lag) % 2


def count(n):
    return max(n, 0) if isinstance(n, int) else n


def xattn_moe_kernel(nc, x, ctx_t, wq_t, wk_t, wv_t, wo_t, bq, bk, bv, bo, sup_t, rup_t, sdown, rdown, router_t,
                     ident, ident_bf, future, spread, expert_no, head_rows, out):
    NB, S, E = x.shape
    T = NB * S
    H, DH = 16, 8
    QB = S // P
    G, J = 4, 4
    UNITS = 12
    NR, TOPK = router_t.shape[1], 4
    NCH = (sup_t.shape[1] + rup_t.shape[1]) // P
    NTT = T // P
    NCT = T // BANK
    PAIRS = ((0, 3), (0, 4), (0, 5), (1, 3), (1, 4), (2, 3))
    MROWS, MROW0 = 2, 96
    VW = 32
    VSTEP = VW // DH
    LAST_LAG = 4
    X_PARTS = ((0, 2), (2, 4), (4, 8), (8, 12), (12, 16))
    QK_TICK = 1

    x_v = x.rearrange("b (t p) e -> p (b t) e", p=P)
    out_v = out.rearrange("b (t p) e -> p (b t) e", p=P)

    with ExitStack() as stack:
        def sb(name, shape, dt):
            return stack.enter_context(nc.sbuf_tensor("sb_" + name, shape, dt))

        def sem(name):
            return stack.enter_context(nc.semaphore("s_" + name))

        psum = stack.enter_context(nc.psum_tensor("psum", [P, 8, BANK], F32))
        BANK_M, MB, BANK_S, SB, BANK_PV, BANK_A, BANK_B = 0, 3, 3, 2, 5, 6, 7

        id_f = sb("id_f", [P, P], F32)
        id_b = sb("id_b", [P, P], BF16)
        fut = sb("fut", [P, P], BF16)
        spr = sb("spr", [3 * NR, NCH - 1, P], BF16)
        hrow = sb("hrow", [H, P], F32)
        exno = sb("exno", [P, NR], F32)
        wq_sb = sb("wq", [E, P], F32)
        wk_sb = sb("wk", [E, P], F32)
        wv_sb = sb("wv", [E, P], F32)
        wo_sb = sb("wo", [P, E], F32)
        rw_sb = sb("rw", [E, NR], F32)
        bq_sb = sb("bq", [P, 1], F32)
        bk_sb = sb("bk", [P, 1], F32)
        bv_sb = sb("bv", [P, 1], F32)
        bv_all = sb("bv_all", [P, P], F32)
        bo_sb = sb("bo", [P, P], F32)
        up_h = sb("up_h", [E, NCH * P], F32R)
        up_l = sb("up_l", [E, NCH * P], F32R)
        dn_h = sb("dn_h", [P, NCH * E], F32R)
        dn_l = sb("dn_l", [P, NCH * E], F32R)
        zero = sb("zero", [P, 1], F32)
        first_exp = sb("first_exp", [P, 1], F32)
        ones_b = sb("ones_b", [MROWS * H, S], BF16)

        x2 = sb("x2", [P, NTT, E], F32)
        xn = sb("xn", [P, NTT, E], F32)
        xn_t = sb("xn_t", [E, T], F32)
        st1 = sb("st1", [P, NTT, 6], F32)
        mv1 = sb("mv1", [P, NTT, 2], F32)
        var1 = sb("var1", [P, NTT], F32)
        rs1 = sb("rs1", [P, NTT], F32)
        halfs = sb("halfs", [P, NTT], F32)
        ctx2 = [sb(f"ctx{s}", [E, S], F32) for s in range(2)]

        qk2 = [sb(f"qk{s}", [P, 6, S], BF16) for s in range(2)]
        qk_res = sb("qk_res", [P, 2, S], F32)
        qk_op = [sb(f"qk_op{s}", [P, H, 2, S], BF16) for s in range(2)]
        q_op, k_op = [o[:, :, 0, :] for o in qk_op], [o[:, :, 1, :] for o in qk_op]
        v_op = [sb(f"v_op{s}", [P, QB, H, VW], F32) for s in range(2)]
        mx = [sb(f"mx{s}", [P, QB, H], F32) for s in range(2)]
        m_parts = [sb(f"m_parts{h}", [P, QB, MROWS, H // 2], BF16) for h in range(2)]
        m_t = [sb(f"m_t{h}", [MROWS * H // 2, S], BF16) for h in range(2)]
        probs = [sb(f"probs{g}", [P, J * S + J * P], F32) for g in range(G)]
        up_f, dn_f = probs[2][:, 0:NCH * P], probs[3][:, 0:NCH * E]
        o_raw = sb("o_raw", [P, G, S], F32)
        num = sb("num", [P, S], F32)
        den = sb("den", [P, H * S // P], F32)
        rden = sb("rden", [P, H * S // P], F32)
        rden_h = sb("rden_h", [H, S], F32)
        att = sb("att", [P, S], F32)

        st2 = sb("st2", [P, QB, 6], F32)
        mv2 = sb("mv2", [P, QB, 2], F32)
        var2 = sb("var2", [P, QB], F32)
        rs2 = sb("rs2", [P, QB], F32)
        xn2 = sb("xn2", [P, QB, E], F32)
        xn2_t = sb("xn2_t", [E, S], F32)
        xh = sb("xh", [E, T], F32R)
        xl = sb("xl", [E, T], F32R)
        top = sb("top", [P, QB, 8], F32)
        top_i = sb("top_i", [P, QB, 8], U32)
        lgm = sb("lgm", [P, QB, NR], F32)
        ex = sb("ex", [P, QB, NR], F32)
        exs = sb("exs", [P, QB], F32)
        rexs = sb("rexs", [P, QB], F32)
        is_top = sb("is_top", [P, QB, NR, TOPK], F32)
        chosen = sb("chosen", [P, QB, NR], F32)
        gsel = sb("gsel", [P, QB, NR], F32)
        gate = sb("gate", [P, QB, NR], F32)
        gres = sb("gres", [P, QB, NR], F32)
        g_parts = sb("g_parts", [P, QB, 3, NR], BF16)
        gate_t = sb("gate_t", [3 * NR, T], BF16)

        UP_BANKS, NF = 3, 4
        DOWN_LAG = 3
        gel = [probs[2 * (n // 3)][:, BANK * (n % 3):BANK * (n % 3) + BANK] for n in range(NF + 1)]
        hid = [probs[2 * (n // 3) + 1][:, BANK * (n % 3):BANK * (n % 3) + BANK] for n in range(NF + 1)]
        buf = [k % NF for k in range(NCH - 1)] + [NF]
        hid_h = [sb(f"hid_h{n}", [P, BANK], F32R) for n in range(NF + 1)]
        hid_l = [sb(f"hid_l{n}", [P, BANK], F32R) for n in range(NF + 1)]
        y_t = o_raw[:, 0:2, :].rearrange("p g q -> p (g q)")
        y = o_raw[:, 2:4, :].rearrange("p g (a e) -> p (g a) e", e=E)

        x_in = [sem(f"x_in{q}") for q in range(len(X_PARTS))]
        id_in, w_in, c_in, ff_in = sem("id_in"), sem("w_in"), sem("c_in"), sem("ff_in")
        zero_set, half_set, ones_set, ones_in, v_ones_set = (sem("zero_set"), sem("half_set"), sem("ones_set"),
                                                             sem("ones_in"), sem("v_ones_set"))
        zeros_set = [sem(f"zeros_set{s}") for s in range(2)]
        stats1, rstd1, xn_done, xnt_ps, xnt_read = sem("stats1"), sem("rstd1"), sem("xn_done"), sem("xnt_ps"), sem("xnt_read")
        resid = sem("resid")
        bv_spread, bv_ps, bo_done = sem("bv_spread"), sem("bv_ps"), sem("bo_done")
        w_hi, w_lo = sem("w_hi"), sem("w_lo")
        ctx_in, ctx1_in = sem("ctx_in"), sem("ctx1_in")
        qk_ps, qk_hi, qk_less = sem("qk_ps"), sem("qk_hi"), sem("qk_less")
        qk_mid, qk_lo = sem("qk_mid"), sem("qk_lo")
        op_in = [sem(f"op_in{h}") for h in range(2)]
        v_ps, v_read = sem("v_ps"), sem("v_read")
        m_ps, m_max = sem("m_ps"), sem("m_max")
        m_split, mt_ps, mt_read = sem("m_split"), sem("mt_ps"), sem("mt_read")
        m_in = [sem(f"m_in{h}") for h in range(2)]
        s_ps, s_exp, s_mask = sem("s_ps"), sem("s_exp"), sem("s_mask")
        pv_ps, pv_read = sem("pv_ps"), sem("pv_read")
        num_in, den_in, rden_in = sem("num_in"), sem("den_in"), sem("rden_in")
        den_inv, rden_ps, att_done, o_ps, x2_done = sem("den_inv"), sem("rden_ps"), sem("att_done"), sem("o_ps"), sem("x2_done")
        stats2, rstd2, xn2_done = sem("stats2"), sem("rstd2"), sem("xn2_done")
        xn2t_ps, xn2t_read, xh_done, xl_done = sem("xn2t_ps"), sem("xn2t_read"), sem("xh_done"), sem("xl_done")
        r_ps, r_exp, r_step = sem("r_ps"), sem("r_exp"), sem("r_step")
        g_step, g_last = sem("g_step"), sem("g_last")
        gt_ps, gt_read = sem("gt_ps"), sem("gt_read")
        u_ps, gate_ps, u_gelu, hid_done = sem("u_ps"), sem("gate_ps"), sem("u_gelu"), sem("hid_done")
        hid_hi, hid_lo, d_ps, d_read, y_ps, y_done = (sem("hid_hi"), sem("hid_lo"), sem("d_ps"), sem("d_read"),
                                                      sem("y_ps"), sem("y_done"))
        out_done, unused = sem("out_done"), sem("unused")
        RSTEPS = 11

        block = stack.enter_context(nc.Block())

        def apart(eng):
            eng.sem_inc(unused, 1)

        def attention(eng, turn_of):
            for i in range(LAST_LAG):
                turn_of(Turn(i, i, NB))
            with eng.Fori(0, (NB - LAST_LAG) // 2) as k:
                for u in range(2):
                    turn_of(Turn(k * 2 + (LAST_LAG + u), LAST_LAG + u, NB))
            for i in range(NB, NB + LAST_LAG):
                turn_of(Turn(i, i, NB))

        early_units = ((8, 10), (1, 2, 4, 6, 8, 10), (0, 1, 2, 4, 6, 7, 8, 9, 10))
        early = {at: m for m, at in enumerate([(NB + 1 + i, t) for i, units in enumerate(early_units) for t in units])}

        def early_chunk(turn, t):
            m = early.get((turn.at, t)) if isinstance(turn.at, int) else None
            return None if m is None else divmod(m, NCH)

        def last_scores(turn):
            return isinstance(turn.at, int) and turn.at == NB + 1

        def exp_units(turn, t):
            return [n for n in (2 * t, 2 * t + 1) if n < UNITS] if last_scores(turn) else [t]

        def sums(turn, t):
            c2, c3 = turn.batch(2), turn.batch(3)
            if last_scores(turn):
                steps = {1: [(c3, 3)], 3: [(c2, 0)], 4: [(c2, 1)], 6: [(c2, 2)], 7: [(c2, 3)]}
            elif isinstance(turn.at, int) and turn.at > NB + 1:
                steps = {}
            else:
                steps = {1: [(c3, 3)], 5: [(c2, 0)], 8: [(c2, 1)], 11: [(c2, 2)]}
            return [(c, g) for c, g in steps.get(t, []) if c is not None]

        def sums_read(turn, t):
            c2, c3 = turn.batch(2), turn.batch(3)
            if last_scores(turn):
                steps = {1: [(c3, 1)], 5: [(c2, 0)], 8: [(c2, 1)]}
            elif isinstance(turn.at, int) and turn.at > NB + 1:
                steps = {}
            else:
                steps = {1: [(c3, 1)], 9: [(c2, 0)]}
            return [(c, n) for c, n in steps.get(t, []) if c is not None]

        def projection(turn, t, unit):
            if isinstance(turn.at, int) and turn.at < 2:
                return {(0, unit): Turn(0, 0, NB), (0, UNITS - 1): Turn(1, 1, NB)}.get((turn.at, t))
            return turn if t == unit and turn.batch(0) is not None else None

        xn_units = {(0, 9): 1, (1, 4): 2, (1, 7): 3, (1, 10): 4}

        users = {
            BANK_A: [("qk", 0, qk_less, 2, 2), ("router", 4, r_step, RSTEPS, 5), ("v", 1, v_read, 1, 1), ("gates", 4, gt_read, 1, 2)],
            BANK_B: [("max1", 2, mt_read, 2, 2), ("xn2", 4, xh_done, 1, 1), ("max0", 1, mt_read, 2, 1), ("rden", 3, att_done, 1, 1),
                     ("o", 3, x2_done, 1, 1)],
        }

        def bank_free(turn, bank, step):
            order = users[bank]
            at = [u[0] for u in order].index(step)
            for back in range(1, 3 * len(order)):
                name, lag, reader, per, which = order[(at - back) % len(order)]
                c = Turn(turn.at - (0 if back <= at else 1 + (back - at - 1) // len(order)), 0, NB).batch(lag)
                if c is not None:
                    return reader, count(per * c + which)
            return None

        @block.sync
        def _(sp):
            def load_x(q):
                tiles = slice(*X_PARTS[q])
                sp.dma_start(x2[:, tiles, :], x_v[:, tiles, :]).then_inc(x_in[q], 16)

            def load_ctx(c, side, done):
                start = c * S
                sp.dma_start(ctx2[side][:, :], ctx_t[:, bass.ds(start, S)]).then_inc(done, 16)

            load_x(0)
            sp.dma_start(id_f[:, :], ident).then_inc(id_in, 16)
            for dst, src in ((wq_sb, wq_t), (wk_sb, wk_t), (bq_sb, bq), (bk_sb, bk)):
                sp.dma_start(dst[:, :], src).then_inc(w_in, 16)

            def operands(c, side, half):
                heads = slice(half * H // 2, (half + 1) * H // 2)
                rows = slice(half * P // 2, (half + 1) * P // 2)
                if isinstance(c, int) and c < 2:
                    sp.wait_ge(zeros_set[side], 2)
                sp.wait_ge(qk_lo, count(c + 1))
                if isinstance(c, int) and c == 1:
                    sp.wait_ge(m_ps, UNITS // 2 * half + 1)
                apart(sp)
                sp.wait_ge(s_ps, count(UNITS * (c - 2) + UNITS // 2 * (half + 1)))
                qk = qk2[side]
                for n, (a, b) in enumerate(PAIRS):
                    sp.dma_start(qk_op[side][DH * n:DH * n + DH, heads, :, :], qk[rows, a:b + 1:b - a, :]).then_inc(op_in[half], 16)

            def maxima(c, side, half):
                heads = slice(half * H // 2, (half + 1) * H // 2)
                sp.wait_ge(mt_read, count(2 * c + 1 + half))
                sp.dma_start(q_op[side][MROW0:MROW0 + MROWS, heads, :], m_t[half][:, :]).then_inc(m_in[half], 16)

            def turn_of(turn):
                c = turn.batch(0)
                if c is not None and not (isinstance(c, int) and c < 2):
                    sp.wait_ge(v_ps, count(c - 1))
                    apart(sp)
                    load_ctx(c, turn.side(0), ctx_in)
                if isinstance(c, int) and c == 0:
                    load_ctx(0, 0, ctx_in)
                    load_x(1)
                    load_ctx(1, 1, ctx1_in)
                    for dst, src in ((id_b, ident_bf), (fut, future), (wv_sb, wv_t), (bv_sb, bv), (wo_sb, wo_t),
                                     (rw_sb, router_t), (hrow, head_rows), (exno, expert_no.partition_broadcast(P)),
                                     (bo_sb, bo.partition_broadcast(P))):
                        sp.dma_start(dst[:, :], src).then_inc(c_in, 16)
                    for q in range(2, len(X_PARTS)):
                        load_x(q)
                    for dst, src in ((up_f[:, 0:P], sup_t), (up_f[:, P:NCH * P], rup_t), (dn_f[:, 0:E], sdown),
                                     (dn_f[:, E:NCH * E].rearrange("p (c h) -> p c h", h=E), rdown), (spr[:, :, :], spread)):
                        sp.dma_start(dst, src).then_inc(ff_in, 16)
                c = turn.batch(1)
                if c is not None:
                    operands(c, turn.side(1), 1)
                c = turn.batch(2)
                if c is not None:
                    maxima(c, turn.side(2), 1)
                c = turn.batch(3)
                if c is not None:
                    sp.wait_ge(pv_read, count(2 * c + 2))
                    sp.wait_ge(den_inv, count(c))
                    sp.dma_start(den[:, :], o_raw[1:P:VW, :, :]).then_inc(den_in, 16)
                    sp.wait_ge(att_done, count(c))
                    sp.dma_start(num[:, :], o_raw[0:P:VSTEP, :, :]).then_inc(num_in, 16)
                c = turn.batch(3)
                if c is not None:
                    sp.wait_ge(den_inv, count(c + 1))
                    sp.wait_ge(rden_ps, count(c))
                    sp.dma_start(rden_h[:, :], rden[:, :]).then_inc(rden_in, 16)
                c = turn.batch(0)
                if c is not None:
                    operands(c, turn.side(0), 0)
                c = turn.batch(1)
                if c is not None:
                    maxima(c, turn.side(1), 0)

            attention(sp, turn_of)

            with sp.Fori(0, NCT) as n:
                sp.wait_ge(y_done, n + 2)
                apart(sp)
                sp.dma_start(out_v[:, bass.ds(n * (BANK // P), BANK // P), :], y).then_inc(out_done, 16)
            sp.wait_ge(out_done, 16 * (NCT + 1))

        @block.gpsimd
        def _(pool):
            nc.gpsimd.memset(zero[:, :], 0.0).then_inc(zero_set, 1)
            nc.gpsimd.memset(halfs[:, :], -0.5).then_inc(half_set, 1)
            nc.gpsimd.memset(ones_b[:, :], 1.0).then_inc(ones_set, 1)

            def rstd_1(q):
                tiles = slice(*X_PARTS[q])
                pool.wait_ge(stats1, 2 * tiles.stop)
                nc.gpsimd.tensor_scalar(var1[:, tiles], mv1[:, tiles, 1], 1e-5, None, ALU.add).then_inc(rstd1, 1)
                pool.wait_ge(rstd1, 2 * q + 1)
                nc.gpsimd.tensor_tensor(rs1[:, tiles], var1[:, tiles], halfs[:, tiles], ALU.pow).then_inc(rstd1, 1)

            def lo_part(dst, full, high, n=slice(None)):
                return nc.gpsimd.tensor_tensor(dst[:, n], full[:, n], high[:, n].bitcast(F32), ALU.subtract)

            def select(c, t):
                g, u = divmod(t, 3)
                pool.wait_ge(s_exp, count(UNITS * c + t + 1))
                apart(pool)
                if u < 2:
                    v = probs[g][:, u * BANK:(u + 1) * BANK].rearrange("p (j q) -> p j q", j=2)[:, :, 0:P]
                else:
                    v = probs[g][:, J * S:J * S + J * P].rearrange("p (j q) -> p j q", j=J)
                nc.gpsimd.affine_select(out=v, in_=v, compare_op=ALU.is_ge, fill=0.0, base=0,
                                        pattern=[[0, v.shape[1]], [1, P]], channel_multiplier=-1).then_inc(s_mask, 1)

            def add_bo(q):
                tiles = slice(4 * q, 4 * q + 4)
                pool.wait_ge(xn_done, 4 * q + 4)
                pool.wait_ge(bo_done, 1)
                nc.gpsimd.tensor_tensor(x2[:, tiles, :], x2[:, tiles, :],
                                        bo_sb[:, :].unsqueeze(1).to_broadcast([P, 4, E]), ALU.add).then_inc(resid, 1)

            def project(turn):
                c = turn.batch(0)
                qk = qk2[turn.side(0)]
                pool.wait_ge(qk_mid, count(c + 1))
                nc.gpsimd.tensor_tensor(qk[:, 2:6:3, :], qk_res[:, :, :], qk[:, 1:5:3, :], ALU.subtract).then_inc(qk_lo, 1)

            def turn_of(turn):
                for t in range(UNITS):
                    c = turn.batch(4)
                    if t == 0 and c is not None:
                        pool.wait_ge(stats2, count(4 * c + 4))
                        apart(pool)
                        nc.gpsimd.tensor_scalar(var2[:, :], mv2[:, :, 1], 1e-5, None, ALU.add).then_inc(rstd2, 1)
                        pool.wait_ge(rstd2, count(2 * c + 1))
                        nc.gpsimd.tensor_tensor(rs2[:, :], var2[:, :], halfs[:, 0:QB], ALU.pow).then_inc(rstd2, 1)
                    if t == 10 and c is not None:
                        pool.wait_ge(r_step, count(RSTEPS * (c + 1)))
                        apart(pool)
                        nc.gpsimd.tensor_copy(g_parts[:, :, 0, :], gate[:, :, :]).then_inc(g_step, 1)
                        pool.wait_ge(g_step, count(3 * c + 1))
                        nc.gpsimd.tensor_tensor(gres[:, :, :], gate[:, :, :], g_parts[:, :, 0, :], ALU.subtract).then_inc(g_step, 1)
                        pool.wait_ge(g_step, count(3 * c + 2))
                        apart(pool)
                        nc.gpsimd.tensor_copy(g_parts[:, :, 1, :], gres[:, :, :]).then_inc(g_step, 1)
                        pool.wait_ge(g_step, count(3 * c + 3))
                        nc.gpsimd.tensor_tensor(g_parts[:, :, 2, :], gres[:, :, :], g_parts[:, :, 1, :], ALU.subtract)\
                            .then_inc(g_last, 1)
                    c = turn.batch(2)
                    if c is not None:
                        for n in exp_units(turn, t):
                            select(c, n)
                    if isinstance(turn.at, int) and turn.at == 2 and t % 3 == 2:
                        add_bo(t // 3)
                    if isinstance(turn.at, int) and (turn.at, t) == (0, 9):
                        for q in range(2, len(X_PARTS)):
                            rstd_1(q)
                    p = projection(turn, t, QK_TICK + 1)
                    if p is not None:
                        project(p)
                    c = turn.batch(4)
                    if t == 6 and c is not None:
                        pool.wait_ge(xh_done, count(c + 1))
                        nc.gpsimd.tensor_tensor(xl[:, bass.ds(c * S, S)], xn2_t[:, :],
                                                xh[:, bass.ds(c * S, S)].bitcast(F32), ALU.subtract).then_inc(xl_done, 1)
                if not isinstance(turn.at, int):
                    return
                if turn.at == 0:
                    pool.wait_ge(ones_set, 1)
                    for side in range(2):
                        pool.wait_ge(zeros_set[side], 2)
                        pool.dma_start(k_op[side][MROW0:MROW0 + MROWS, :, :], ones_b[:, :]).then_inc(ones_in, 16)
                    pool.wait_ge(w_hi, 1)
                    lo_part(up_l, up_f, up_h).then_inc(w_lo, 1)
                if turn.at == 1:
                    pool.wait_ge(w_hi, 2)
                    lo_part(dn_l, dn_f, dn_h).then_inc(w_lo, 1)

            pool.wait_ge(half_set, 1)
            nc.gpsimd.memset(qk_op[0][:, 0:H // 2, :, :].bitcast(F32), 0.0).then_inc(zeros_set[0], 1)
            rstd_1(0)
            nc.gpsimd.memset(qk_op[0][:, H // 2:H, :, :].bitcast(F32), 0.0).then_inc(zeros_set[0], 1)
            rstd_1(1)
            attention(pool, turn_of)

        @block.scalar
        def _(act):
            act.sem_inc(gt_read, 1)

            def zeros_1(half):
                nc.scalar.copy(qk_op[1][:, half * H // 2:(half + 1) * H // 2, :, :].rearrange("p h n s -> p (h n s)"),
                               zero[:, :].to_broadcast([P, H * S])).then_inc(zeros_set[1], 1)

            act.wait_ge(zero_set, 1)
            nc.scalar.activation(first_exp[:, :], zero[:, :], ACT.Exp).then_inc(unused, 1)
            zeros_1(0)

            def gelu(n, k):
                at = n * NCH + k
                act.wait_ge(u_ps, at + 1)
                act.wait_ge(hid_done, count(at - NF + 1))
                nc.scalar.activation(gel[buf[k]], psum[:, k % UP_BANKS, :], ACT.Gelu).then_inc(u_gelu, 1)

            def high(n, k):
                at = n * NCH + k
                act.wait_ge(hid_done, at + 1)
                act.wait_ge(d_ps, count(at - NF + 1))
                nc.scalar.copy(hid_h[buf[k]][:, :], hid[buf[k]]).then_inc(hid_hi, 1)

            def read_d(n):
                act.wait_ge(d_ps, (n + 1) * NCH)
                act.wait_ge(y_ps, n + 1)
                nc.scalar.copy(y_t, psum[:, 5, :]).then_inc(d_read, 1)

            def chunk(n, k, first):
                gelu(n, k)
                if k > 0:
                    high(n, k - 1)
                elif not first:
                    high(n - 1, NCH - 1)
                if k == DOWN_LAG - 1 and not first:
                    read_d(n - 1)

            def read_xn(q):
                act.wait_ge(xnt_ps, q + 1)
                a, b = X_PARTS[q]
                nc.scalar.copy(xn_t[:, P * a:P * b], psum[:, BANK_PV - q % 2, 0:P * (b - a)]).then_inc(xnt_read, 1)

            def read_pv(c, n):
                act.wait_ge(pv_ps, count(G * c + 2 * n + 2))
                act.wait_ge(num_in, count(16 * c))
                act.wait_ge(den_in, count(16 * c))
                nc.scalar.copy(o_raw[:, 2 * n:2 * n + 2, :].rearrange("p g q -> p (g q)"), psum[:, BANK_PV, :])\
                    .then_inc(pv_read, 1)

            def read_maxima(c, half):
                act.wait_ge(mt_ps, count(2 * c + 1 + half))
                act.wait_ge(m_in[half], count(16 * c))
                nc.scalar.copy(m_t[half][:, :], psum[0:MROWS * H // 2, BANK_B, 0:S // 2].bitcast(BF16)).then_inc(mt_read, 1)

            def project(turn):
                c = turn.batch(0)
                act.wait_ge(qk_ps, count(c + 1))
                for half in range(2):
                    act.wait_ge(op_in[half], count(96 * (c - 1)))
                if isinstance(c, int) and c == 0:
                    act.wait_ge(w_in, 64)
                for n, bias in enumerate((bq_sb, bk_sb)):
                    nc.scalar.activation(qk2[turn.side(0)][:, 3 * n, :], psum[:, BANK_A, S * n:S * n + S], ACT.Identity,
                                         bias=bias[:, :]).then_inc(qk_hi, 1)

            def turn_of(turn):
                for t in range(UNITS):
                    c = turn.batch(2)
                    for n in exp_units(turn, t) if c is not None else []:
                        g, u = divmod(n, 3)
                        act.wait_ge(s_ps, count(UNITS * c + n + 1))
                        nc.scalar.activation(probs[g][:, u * BANK:(u + 1) * BANK], psum[:, BANK_S + n % SB, :], ACT.Exp,
                                             scale=float(DH) ** -0.5).then_inc(s_exp, 1)
                    if t == 0 and c is not None:
                        read_maxima(c, 1)
                    for c, n in sums_read(turn, t):
                        read_pv(c, n)
                    if isinstance(turn.at, int) and (turn.at, t) == (0, 9):
                        zeros_1(1)
                    p = projection(turn, t, QK_TICK)
                    if p is not None:
                        project(p)
                    c = turn.batch(4)
                    if t == 3 and c is not None:
                        act.wait_ge(xn2t_ps, count(c + 1))
                        nc.scalar.copy(xn2_t[:, :], psum[:, BANK_B, 0:S]).then_inc(xn2t_read, 1)
                        nc.scalar.copy(xh[:, bass.ds(c * S, S)], psum[:, BANK_B, 0:S]).then_inc(xh_done, 1)
                    c = turn.batch(1)
                    if t == 7 and c is not None:
                        read_maxima(c, 0)
                    c = turn.batch(4)
                    if t == 7 and c is not None:
                        act.wait_ge(r_step, count(RSTEPS * c + 5))
                        nc.scalar.activation(ex[:, :, :], lgm[:, :, :], ACT.Exp).then_inc(r_exp, 1)
                    c = turn.batch(1)
                    if t == 10 and c is not None:
                        act.wait_ge(v_ps, count(c + 1))
                        act.wait_ge(pv_ps, count(G * (c - 1)))
                        if isinstance(c, int) and c < 2:
                            act.wait_ge(v_ones_set, 2)
                        nc.scalar.copy(v_op[turn.side(1)][:, :, :, 0:VW:VSTEP],
                                       psum[:, BANK_A, 0:QB * P].rearrange("p (a h d) -> p a h d", a=QB, h=H)).then_inc(v_read, 1)
                    c = turn.batch(4)
                    if t == 11 and c is not None:
                        act.wait_ge(gt_ps, count(c + 1))
                        nc.scalar.copy(gate_t[:, bass.ds(c * S, S)], psum[0:3 * NR, BANK_A, 0:S // 2].bitcast(BF16))\
                            .then_inc(gt_read, 1)
                    if isinstance(turn.at, int) and (turn.at, t) in xn_units:
                        read_xn(xn_units[turn.at, t])
                    at = early_chunk(turn, t)
                    if at == (1, 0):
                        act.wait_ge(num_in, 16 * NB)
                        act.wait_ge(den_in, 16 * NB)
                    if at is not None:
                        chunk(*at, at[0] == 0)
                if not isinstance(turn.at, int):
                    return
                if turn.at == 0:
                    act.wait_ge(ff_in, 16 * 5)
                    nc.scalar.copy(up_h[:, :], up_f).then_inc(w_hi, 1)
                    nc.scalar.copy(dn_h[:, :], dn_f).then_inc(w_hi, 1)
                if turn.at == 1:
                    act.wait_ge(w_lo, 2)

            read_xn(0)
            attention(act, turn_of)

            for k in range(len(early) - NCH, NCH):
                chunk(1, k, False)
            with act.Fori(2, NCT) as n:
                for k in range(NCH):
                    chunk(n, k, False)
            high(NCT - 1, NCH - 1)
            read_d(NCT - 1)

        @block.vector
        def _(dve):
            def gated(n, k):
                at = n * NCH + k
                dve.wait_ge(u_gelu, at + 1)
                dve.wait_ge(hid_lo, count(at - NF + 1))
                if k == 0:
                    nc.vector.tensor_copy(hid[buf[k]], gel[buf[k]]).then_inc(hid_done, 1)
                else:
                    dve.wait_ge(gate_ps, (NCH - 1) * n + k)
                    nc.vector.tensor_tensor(hid[buf[k]], gel[buf[k]], psum[:, 3 + k % 2, :], ALU.mult)\
                        .then_inc(hid_done, 1)

            def low(n, k):
                at = n * NCH + k
                dve.wait_ge(hid_hi, at + 1)
                dve.wait_ge(d_ps, count(at - NF + 1))
                nc.vector.tensor_tensor(hid_l[buf[k]][:, :], hid[buf[k]], hid_h[buf[k]][:, :].bitcast(F32),
                                        ALU.subtract).then_inc(hid_lo, 1)

            def finish(n):
                dve.wait_ge(y_ps, n + 2)
                dve.wait_ge(out_done, 16 * (n + 1))
                nc.vector.tensor_tensor(y, psum[:, BANK_B, :].rearrange("p (a e) -> p a e", e=E),
                                        x2[:, bass.ds(n * (BANK // P), BANK // P), :], ALU.add).then_inc(y_done, 1)

            def chunk(n, k, first):
                gated(n, k)
                if k > 0:
                    low(n, k - 1)
                elif not first:
                    low(n - 1, NCH - 1)
                if k == DOWN_LAG + 1 and not first:
                    finish(n - 1)

            def stats_1(q):
                tiles = range(*X_PARTS[q])
                dve.wait_ge(x_in[q], 16)
                for a in tiles:
                    nc.vector.bn_stats(st1[:, a, :], x2[:, a, :]).then_inc(stats1, 1)
                for n, a in enumerate(tiles):
                    dve.wait_ge(stats1, 2 * tiles[0] + n + 1)
                    nc.vector.bn_aggr(mv1[:, a, :], st1[:, a, :]).then_inc(stats1, 1)
                dve.wait_ge(stats1, 2 * tiles[-1] + 2)

            def apply_1(q):
                dve.wait_ge(rstd1, 2 * q + 2)
                for a in range(*X_PARTS[q]):
                    nc.vector.tensor_scalar(xn[:, a, :], x2[:, a, :], mv1[:, a, 0:1], rs1[:, a:a + 1],
                                            ALU.subtract, ALU.mult).then_inc(xn_done, 1)

            def split_maxima(c, side, half):
                heads = slice(half * H // 2, (half + 1) * H // 2)
                m = mx[side][:, :, heads]
                high, low = (m_parts[half][:, :, n, :] for n in range(2))
                dve.wait_ge(m_max, count(UNITS * c + UNITS // 2 * (half + 1)))
                dve.wait_ge(mt_ps, count(2 * c - 1 + half))
                nc.vector.tensor_scalar(high, m, -1.0, None, ALU.mult).then_inc(m_split, 1)
                dve.wait_ge(m_split, count(4 * c + 2 * half + 1))
                nc.vector.scalar_tensor_tensor(low, m, -1.0, high, ALU.mult, ALU.subtract).then_inc(m_split, 1)

            def choose(c, t):
                def after(n):
                    dve.wait_ge(r_step, count(RSTEPS * c + n))

                lg = psum[:, BANK_A, 0:QB * NR].rearrange("p (a r) -> p a r", a=QB)
                if t == 6:
                    dve.wait_ge(r_ps, count(c + 1))
                    apart(dve)
                    for a in range(QB):
                        nc.vector.max(top[:, a, :], lg[:, a, :]).then_inc(r_step, 1)
                    after(2)
                    apart(dve)
                    for a in range(QB):
                        nc.vector.max_index(top_i[:, a, :], top[:, a, :], lg[:, a, :]).then_inc(r_step, 1)
                    nc.vector.tensor_tensor(lgm[:, :, :], lg, top[:, :, 0:1].to_broadcast([P, QB, NR]), ALU.subtract)\
                        .then_inc(r_step, 1)
                if t == 7:
                    after(4)
                    nc.vector.tensor_tensor(
                        is_top[:, :, :, :], exno[:, :].unsqueeze(1).unsqueeze(3).to_broadcast([P, QB, NR, TOPK]),
                        top_i[:, :, 0:TOPK].unsqueeze(2).to_broadcast([P, QB, NR, TOPK]), ALU.is_equal).then_inc(r_step, 1)
                if t == 8:
                    after(6)
                    nc.vector.tensor_reduce(chosen[:, :, :], is_top[:, :, :, :], AX, ALU.add).then_inc(r_step, 1)
                    dve.wait_ge(r_exp, count(c + 1))
                    nc.vector.tensor_reduce(exs[:, :], ex[:, :, :], AX, ALU.add).then_inc(r_step, 1)
                if t == 9:
                    after(8)
                    nc.vector.reciprocal(rexs[:, :], exs[:, :]).then_inc(r_step, 1)
                    nc.vector.tensor_tensor(gsel[:, :, :], ex[:, :, :], chosen[:, :, :], ALU.mult).then_inc(r_step, 1)
                    after(10)
                    nc.vector.tensor_tensor(gate[:, :, :], gsel[:, :, :], rexs[:, :].unsqueeze(2).to_broadcast([P, QB, NR]),
                                            ALU.mult).then_inc(r_step, 1)

            def project(turn):
                c = turn.batch(0)
                qk = qk2[turn.side(0)]
                dve.wait_ge(qk_lo, count(c))
                dve.wait_ge(qk_hi, count(2 * c + 2))
                for n, bias in enumerate((bq_sb, bk_sb)):
                    nc.vector.scalar_tensor_tensor(qk_res[:, n, :], psum[:, BANK_A, S * n:S * n + S], bias[:, :],
                                                   qk[:, 3 * n, :], ALU.add, ALU.subtract).then_inc(qk_less, 1)
                dve.wait_ge(qk_less, count(2 * c + 2))
                nc.vector.tensor_copy(qk[:, 1:5:3, :], qk_res[:, :, :]).then_inc(qk_mid, 1)

            def turn_of(turn):
                for t in range(UNITS):
                    c = turn.batch(1)
                    if c is not None:
                        g, u = divmod(t, 3)
                        dve.wait_ge(m_ps, count(UNITS * c + t + 1))
                        if u < 2:
                            src = psum[:, BANK_M + t % MB, :].rearrange("p (j k) -> p j k", j=2)
                            dst = mx[turn.side(1)][:, 1, J * g + 2 * u:J * g + 2 * u + 2]
                        else:
                            src = psum[:, BANK_M + t % MB, :].rearrange("p (j k) -> p j k", j=J)
                            dst = mx[turn.side(1)][:, 0, J * g:J * g + J]
                        nc.vector.tensor_reduce(dst, src, AX, ALU.max).then_inc(m_max, 1)
                        if t in (5, 11):
                            split_maxima(c, turn.side(1), t // 6)
                    c = turn.batch(4)
                    if t == 1 and c is not None:
                        dve.wait_ge(rstd2, count(2 * c + 2))
                        for a in range(QB):
                            nc.vector.tensor_scalar(xn2[:, a, :], x2[:, bass.ds(c * QB + a, 1), :].rearrange("p a e -> p (a e)"),
                                                    mv2[:, a, 0:1], rs2[:, a:a + 1], ALU.subtract, ALU.mult)\
                                .then_inc(xn2_done, 1)
                    if isinstance(turn.at, int) and (turn.at, t) == (0, 9):
                        dve.wait_ge(c_in, 16 * 9)
                        nc.vector.tensor_copy(bv_all[:, :], bv_sb[:, :].to_broadcast([P, P])).then_inc(bv_spread, 1)
                        for q in range(2, len(X_PARTS)):
                            stats_1(q)
                    p = projection(turn, t, QK_TICK + 1)
                    if p is not None:
                        project(p)
                    c = turn.batch(4)
                    if t >= 6 and c is not None:
                        choose(c, t)
                    c = turn.batch(3)
                    if t == 4 and c is not None:
                        dve.wait_ge(den_in, count(16 * (c + 1)))
                        dve.wait_ge(rden_in, count(16 * c))
                        nc.vector.reciprocal(rden[:, :], den[:, :]).then_inc(den_inv, 1)
                    if t == 9 and c is not None:
                        dve.wait_ge(rden_ps, count(c + 1))
                        dve.wait_ge(num_in, count(16 * (c + 1)))
                        dve.wait_ge(o_ps, count(c))
                        nc.vector.tensor_tensor(att[:, :], psum[:, BANK_B, 0:S], num[:, :], ALU.mult).then_inc(att_done, 1)
                    c = turn.batch(3)
                    if t == 11 and c is not None:
                        dve.wait_ge(o_ps, count(c + 1))
                        dve.wait_ge(resid, 4)
                        rows = x2[:, bass.ds(c * QB, QB), :]
                        nc.vector.tensor_tensor(rows, psum[:, BANK_B, 0:QB * P].rearrange("p (a e) -> p a e", a=QB), rows,
                                                ALU.add).then_inc(x2_done, 1)
                        dve.wait_ge(x2_done, count(c + 1))
                        dve.wait_ge(rstd2, count(2 * c))
                        apart(dve)
                        for a in range(QB):
                            nc.vector.bn_stats(st2[:, a, :], x2[:, bass.ds(c * QB + a, 1), :].rearrange("p a e -> p (a e)"))\
                                .then_inc(stats2, 1)
                        for a in range(QB):
                            dve.wait_ge(stats2, count(4 * c + a + 1))
                            apart(dve)
                            nc.vector.bn_aggr(mv2[:, a, :], st2[:, a, :]).then_inc(stats2, 1)
                    if isinstance(turn.at, int) and turn.at == 1 and t in (3, 6):
                        apply_1(2 + t // 3)
                    at = early_chunk(turn, t)
                    if at is not None:
                        chunk(*at, at[0] == 0)
                if isinstance(turn.at, int) and turn.at == 0:
                    dve.wait_ge(bv_ps, 1)
                    nc.vector.tensor_tensor(bo_sb[:, :], bo_sb[:, :], psum[:, BANK_B, 0:E], ALU.add).then_inc(bo_done, 1)
                    apply_1(2)

            for side in range(2):
                nc.vector.memset(v_op[side][:, :, :, :], 1.0).then_inc(v_ones_set, 1)
            for q in range(2):
                stats_1(q)
                apply_1(q)
            attention(dve, turn_of)

            for k in range(len(early) - NCH, NCH):
                chunk(1, k, False)
            with dve.Fori(2, NCT) as n:
                for k in range(NCH):
                    chunk(n, k, False)
            low(NCT - 1, NCH - 1)
            finish(NCT - 1)

        @block.tensor
        def _(pe):
            mm = nc.tensor.matmul

            def wait_bank(turn, bank, step):
                got = bank_free(turn, bank, step)
                if got is not None:
                    pe.wait_ge(*got)

            def up(n, k):
                at = n * NCH + k
                cols = bass.ds(n * BANK, BANK)
                w = slice(P * k, P * k + P)
                pe.wait_ge(u_gelu, count(at - UP_BANKS + 1))
                mm(psum[:, k % UP_BANKS, :], up_h[:, w], xh[:, cols], start=True, stop=False)
                mm(psum[:, k % UP_BANKS, :], up_h[:, w], xl[:, cols], start=False, stop=False)
                mm(psum[:, k % UP_BANKS, :], up_l[:, w], xh[:, cols], start=False, stop=True).then_inc(u_ps, 1)
                if k > 0:
                    pe.wait_ge(hid_done, count(at - 1) if isinstance(at, int) else at - 1)
                    apart(pe)
                    mm(psum[:, 3 + k % 2, :], spr[:, k - 1, :], gate_t[:, cols], start=True, stop=True).then_inc(gate_ps, 1)

            def down(n, k):
                at = n * NCH + k
                w = slice(E * k, E * k + E)
                if k == 0:
                    pe.wait_ge(d_read, n)
                pe.wait_ge(hid_hi, at + 1)
                mm(psum[:, 5, :], dn_h[:, w], hid_h[buf[k]][:, :], start=(k == 0), stop=False)
                mm(psum[:, 5, :], dn_l[:, w], hid_h[buf[k]][:, :], start=False, stop=False)
                pe.wait_ge(hid_lo, at + 1)
                mm(psum[:, 5, :], dn_h[:, w], hid_l[buf[k]][:, :], start=False, stop=(k == NCH - 1)).then_inc(d_ps, 1)

            def transpose_y(n):
                pe.wait_ge(d_read, n + 1)
                pe.wait_ge(y_done, n + 1)
                for a in range(BANK // P):
                    last = nc.tensor.transpose(psum[:, BANK_B, P * a:P * a + P], y_t[:, P * a:P * a + P], id_f[:, :])
                last.then_inc(y_ps, 1)

            def chunk(n, k, first):
                up(n, k)
                if k >= DOWN_LAG:
                    down(n, k - DOWN_LAG)
                elif not first:
                    down(n - 1, NCH - DOWN_LAG + k)
                if k == DOWN_LAG and not first:
                    transpose_y(n - 1)

            def transpose_xn(q):
                a, b = X_PARTS[q]
                pe.wait_ge(xn_done, b)
                if q >= 2:
                    pe.wait_ge(xnt_read, q - 1)
                for n in range(b - a):
                    last = nc.tensor.transpose(psum[:, BANK_PV - q % 2, P * n:P * n + P], xn[:, a + n, :], id_f[:, :])
                last.then_inc(xnt_ps, 1)

            def max_unit(c, side, t):
                g, u = divmod(t, 3)
                if t % 6 == 0:
                    pe.wait_ge(op_in[t // 6], count(96 * (c + 1)))
                pe.wait_ge(m_max, count(UNITS * c + t - MB + 1))
                bank = psum[:, BANK_M + t % MB, :]
                if u < 2:
                    heads = [J * g + 2 * u, J * g + 2 * u + 1]
                    v = bank.rearrange("p (j k) -> p j k", j=2)
                    mm(v[:, :, P:2 * P], id_b[:, :], fut[:, :].unsqueeze(1).to_broadcast([P, 2, P]), start=True, stop=False,
                       skip_group_check=True)
                    for n, h in enumerate(heads):
                        last = mm(v[:, n, :], q_op[side][0:MROW0, h, P:2 * P], k_op[side][0:MROW0, h, :], start=False,
                                  stop=(n == 1), skip_group_check=True)
                else:
                    v = bank.rearrange("p (j k) -> p j k", j=J)
                    mm(v, id_b[:, :], fut[:, :].unsqueeze(1).to_broadcast([P, J, P]), start=True, stop=False,
                       skip_group_check=True)
                    for n in range(J):
                        last = mm(v[:, n, :], q_op[side][0:MROW0, J * g + n, 0:P], k_op[side][0:MROW0, J * g + n, 0:P],
                                  start=False, stop=(n == J - 1), skip_group_check=True)
                last.then_inc(m_ps, 1)

            def exp_unit(c, side, t):
                g, u = divmod(t, 3)
                if t % 6 == 0:
                    pe.wait_ge(m_in[t // 6], count(16 * (c + 1)))
                pe.wait_ge(s_exp, count(UNITS * c + t - SB + 1))
                bank = psum[:, BANK_S + t % SB, :]
                if u < 2:
                    for n in range(2):
                        h = J * g + 2 * u + n
                        last = mm(bank[:, S * n:S * n + S], k_op[side][:, h, 0:P], q_op[side][:, h, :], start=True, stop=True)
                else:
                    for n in range(J):
                        h = J * g + n
                        last = mm(bank[:, P * n:P * n + P], k_op[side][:, h, P:2 * P], q_op[side][:, h, P:2 * P],
                                  start=True, stop=True)
                last.then_inc(s_ps, 1)

            def pv(c, side, g):
                pe.wait_ge(s_mask, count(UNITS * c + 3 * g + 3))
                if g == 0:
                    pe.wait_ge(v_read, count(c + 1))
                if g % 2 == 0:
                    pe.wait_ge(pv_read, count(2 * c + g // 2))
                col = S * (g % 2)
                bank = psum[:, BANK_PV, :]
                for j in range(J):
                    mm(bank[32 * j:32 * j + 32, col:col + S], v_op[side][:, 0, J * g + j, :],
                       probs[g][:, S * j:S * j + S], start=True, stop=False)
                for j in range(J):
                    last = mm(bank[32 * j:32 * j + 32, col + P:col + S], v_op[side][:, 1, J * g + j, :],
                              probs[g][:, J * S + P * j:J * S + P * j + P], start=False, stop=True)
                last.then_inc(pv_ps, 1)

            def transpose_maxima(turn, c, half):
                pe.wait_ge(m_split, count(4 * c + 2 * half + 2))
                wait_bank(turn, BANK_B, f"max{half}")
                apart(pe)
                bank = psum[:, BANK_B, :].bitcast(BF16)
                for a in range(QB):
                    last = nc.tensor.transpose(bank[0:MROWS * H // 2, P * a:P * a + P],
                                               m_parts[half][:, a, :, :].rearrange("p m h -> p (m h)"), id_b[:, :])
                last.then_inc(mt_ps, 1)

            def project(turn):
                c = turn.batch(0)
                if isinstance(c, int) and c < 2:
                    pe.wait_ge((ctx_in, ctx1_in)[c], 16)
                else:
                    pe.wait_ge(ctx_in, 16 * c)
                wait_bank(turn, BANK_A, "qk")
                mm(psum[:, BANK_A, S:2 * S], wk_sb[:, :], ctx2[turn.side(0)][:, :], start=True, stop=True)
                if isinstance(c, int) and c == 0:
                    transpose_xn(0)
                if isinstance(c, int):
                    pe.wait_ge(xnt_read, c + 1 if c < 2 else c // 2 + 2)
                mm(psum[:, BANK_A, 0:S], wq_sb[:, :], xn_t[:, bass.ds(c * S, S)], start=True, stop=True).then_inc(qk_ps, 1)

            def turn_of(turn):
                for t in range(UNITS):
                    c = turn.batch(1)
                    if c is not None:
                        max_unit(c, turn.side(1), t)
                    c = turn.batch(2)
                    if c is not None:
                        for n in exp_units(turn, t):
                            exp_unit(c, turn.side(2), n)
                        if t == 0:
                            transpose_maxima(turn, c, 1)
                    for c, g in sums(turn, t):
                        pv(c, turn.side(3 if g == 3 and not (last_scores(turn) and t > 1) else 2), g)
                    p = projection(turn, t, QK_TICK)
                    if p is not None:
                        project(p)
                    c = turn.batch(4)
                    if t == 3 and c is not None:
                        pe.wait_ge(xn2_done, count(QB * (c + 1)))
                        wait_bank(turn, BANK_B, "xn2")
                        for a in range(QB):
                            last = nc.tensor.transpose(psum[:, BANK_B, P * a:P * a + P], xn2[:, a, :], id_f[:, :])
                        last.then_inc(xn2t_ps, 1)
                    if t == 5 and c is not None:
                        pe.wait_ge(xn2t_read, count(c + 1))
                        wait_bank(turn, BANK_A, "router")
                        for a in range(QB):
                            last = mm(psum[:, BANK_A, NR * a:NR * a + NR], xn2_t[:, P * a:P * a + P], rw_sb[:, :],
                                      start=True, stop=True)
                        last.then_inc(r_ps, 1)
                    c = turn.batch(1)
                    if t == 7 and c is not None:
                        transpose_maxima(turn, c, 0)
                    if t == 9 and c is not None:
                        wait_bank(turn, BANK_A, "v")
                        for a in range(QB):
                            last = mm(psum[:, BANK_A, P * a:P * a + P], ctx2[turn.side(1)][:, P * a:P * a + P], wv_sb[:, :],
                                      start=True, stop=True)
                        last.then_inc(v_ps, 1)
                    c = turn.batch(3)
                    if t == 9 and c is not None:
                        pe.wait_ge(rden_in, count(16 * (c + 1)))
                        wait_bank(turn, BANK_B, "rden")
                        mm(psum[:, BANK_B, 0:S], hrow[:, :], rden_h[:, :], start=True, stop=True).then_inc(rden_ps, 1)
                    if t == 11 and c is not None:
                        pe.wait_ge(att_done, count(c + 1))
                        wait_bank(turn, BANK_B, "o")
                        for a in range(QB):
                            last = mm(psum[:, BANK_B, P * a:P * a + P], att[:, P * a:P * a + P], wo_sb[:, :],
                                      start=True, stop=True)
                        last.then_inc(o_ps, 1)
                    c = turn.batch(4)
                    if t == 11 and c is not None:
                        pe.wait_ge(g_last, count(c + 1))
                        wait_bank(turn, BANK_A, "gates")
                        apart(pe)
                        bank = psum[:, BANK_A, :].bitcast(BF16)
                        for a in range(QB):
                            last = nc.tensor.transpose(bank[0:3 * NR, P * a:P * a + P],
                                                       g_parts[:, a, :, :].rearrange("p n r -> p (n r)"), id_b[:, :])
                        last.then_inc(gt_ps, 1)
                    if isinstance(turn.at, int) and (turn.at, t) in xn_units:
                        transpose_xn(xn_units[turn.at, t])
                    at = early_chunk(turn, t)
                    if at == (0, 0):
                        pe.wait_ge(w_lo, 2)
                        pe.wait_ge(ff_in, 16 * 5)
                        pe.wait_ge(xl_done, BANK // S)
                        pe.wait_ge(gt_read, BANK // S + 1)
                        pe.wait_ge(m_max, UNITS * NB)
                        pe.wait_ge(s_exp, UNITS * NB)
                    if at == (0, 1):
                        pe.wait_ge(pv_read, 2 * NB)
                    if at == (1, DOWN_LAG):
                        pe.wait_ge(xh_done, NB)
                    if at == (1, 0):
                        pe.wait_ge(xl_done, 2 * BANK // S)
                        pe.wait_ge(gt_read, 2 * BANK // S + 1)
                    if at is not None:
                        chunk(*at, at[0] == 0)
                if not isinstance(turn.at, int):
                    return
                if turn.at == 0:
                    pe.wait_ge(c_in, 16 * 9)
                    pe.wait_ge(bv_spread, 1)
                    mm(psum[:, BANK_B, 0:E], bv_all[:, :], wo_sb[:, :], start=True, stop=True).then_inc(bv_ps, 1)
                    pe.wait_ge(bo_done, 1)
                if turn.at == 1:
                    pe.wait_ge(ones_in, 32)
                    pe.wait_ge(xnt_read, len(X_PARTS))

            pe.sem_inc(y_ps, 1)
            pe.sem_inc(y_done, 1)
            pe.sem_inc(out_done, 16)
            pe.wait_ge(id_in, 16)
            pe.wait_ge(w_in, 64)
            attention(pe, turn_of)

            pe.wait_ge(xh_done, NB)
            for k in range(len(early) - NCH, NCH):
                chunk(1, k, False)
            pe.wait_ge(xl_done, NB)
            pe.wait_ge(gt_read, NB + 1)
            with pe.Fori(2, NCT) as n:
                for k in range(NCH):
                    chunk(n, k, False)
            for k in range(NCH - DOWN_LAG, NCH):
                down(NCT - 1, k)
            transpose_y(NCT - 1)


def kernel(x, ctx_1024, L0_xattn_Wq, L0_xattn_Wk, L0_xattn_Wv, L0_xattn_Wo, L0_xattn_bq, L0_xattn_bk, L0_xattn_bv,
           L0_xattn_bo, L0_ffn_shared_up, L0_ffn_shared_down, L0_ffn_routed_up, L0_ffn_routed_down, L0_ffn_router_w):
    import concourse.bacc as bacc
    import ml_dtypes
    from concourse.bass_utils import run_bass_kernel_spmd

    nb, s, e = x.shape
    heads, dh = 16, 8
    n = np.arange(e).reshape(2, heads // 2, dh).transpose(0, 2, 1).reshape(-1)
    r = np.arange(e).reshape(4, 4, dh).transpose(1, 2, 0).reshape(-1)
    n_routed, ed, _ = L0_ffn_routed_up.shape
    n_shared = L0_ffn_shared_up.shape[0]
    pairs = n_routed // 2
    spread = np.zeros((3, n_routed, pairs, 128), np.float32)
    for c in range(pairs):
        for half in range(2):
            spread[:, 2 * c + half, c, ed * half:ed * half + ed] = 1.0
    head_rows = np.zeros((heads, 4, dh, 4), np.float32)
    for h in range(heads):
        head_rows[h, h // 4, :, h % 4] = 1.0
    future = np.where(np.arange(128)[None, :] > np.arange(128)[:, None], -1e30, 0.0)
    arrays = {
        "x": x,
        "ctx_t": np.asarray(ctx_1024).reshape(nb * s, e).T,
        "wq_t": np.asarray(L0_xattn_Wq)[n].T,
        "wk_t": np.asarray(L0_xattn_Wk)[n].T,
        "wv_t": np.asarray(L0_xattn_Wv).T,
        "wo_t": np.asarray(L0_xattn_Wo)[:, r].T,
        "bq": np.asarray(L0_xattn_bq)[n][:, None],
        "bk": np.asarray(L0_xattn_bk)[n][:, None],
        "bv": np.asarray(L0_xattn_bv)[r][:, None],
        "bo": L0_xattn_bo,
        "sup_t": np.asarray(L0_ffn_shared_up).reshape(n_shared * ed, e).T,
        "rup_t": np.asarray(L0_ffn_routed_up).reshape(n_routed * ed, e).T,
        "sdown": np.asarray(L0_ffn_shared_down).transpose(0, 2, 1).reshape(n_shared * ed, e),
        "rdown": np.asarray(L0_ffn_routed_down).transpose(0, 2, 1).reshape(pairs, 128, e).transpose(1, 0, 2),
        "router_t": np.asarray(L0_ffn_router_w).T,
        "ident": np.eye(128, dtype=np.float32),
        "ident_bf": np.eye(128).astype(ml_dtypes.bfloat16),
        "future": future.astype(ml_dtypes.bfloat16),
        "spread": spread.reshape(3 * n_routed, pairs, 128).astype(ml_dtypes.bfloat16),
        "expert_no": np.arange(n_routed, dtype=np.float32),
        "head_rows": head_rows.reshape(heads, e),
    }
    nc = bacc.Bacc("TRN2", target_bir_lowering=False, num_devices=1)
    given, args = {}, []
    for name, a in arrays.items():
        a = np.ascontiguousarray(a)
        given[f"in_{name}"] = a
        args.append(nc.dram_tensor(f"in_{name}", a.shape, mybir.dt.from_np(a.dtype), kind="ExternalInput").ap())
    args.append(nc.dram_tensor("out_0", (nb, s, e), mybir.dt.float32, kind="ExternalOutput").ap())
    xattn_moe_kernel(nc, *args)
    got = run_bass_kernel_spmd(nc, [given], core_ids=[0])
    return got.results[0]["out_0"]
```
